# Optimizing a Trainium2 kernel written in Bass

```python
import numpy as np
import jax
import jax.numpy as jnp

def _softmax(x, axis=-1):
    return jax.nn.softmax(x, axis=axis)

def _gelu(x):
    return jax.nn.gelu(x, approximate=True)

def _silu(x):
    return jax.nn.silu(x)

def _sigmoid(x):
    return jax.nn.sigmoid(x)

def _layernorm(x, axis=-1, eps=1e-05):
    m = jnp.mean(x, axis=axis, keepdims=True)
    v = jnp.var(x, axis=axis, keepdims=True)
    return (x - m) / jnp.sqrt(v + eps)

def _scatter_add(tgt, idx, src, axis=0):
    return tgt.at[idx].add(src)

def _segment_sum(src, seg, n):
    return jax.ops.segment_sum(src, seg, n)
kernel_name = 'mk_sandwich_d1_jaxref_r8_e17496'

def setup_inputs(seed: int=0):
    np.random.seed(seed)
    _w = jnp.asarray

    def _L0_attn_setup():
        import math
        import jax, jax.numpy as jnp
        import numpy as np
        N_HEADS = 16
        D_EMBED = 128
        key = jax.random.key(seed)
        ks = jax.random.split(key, 5)
        b, l, d = (2, 256, D_EMBED)
        return {'x': jax.random.normal(ks[0], (b, l, d), dtype=jnp.float32), 'w_in': jax.random.normal(ks[1], (3 * d, d), dtype=jnp.float32) * 0.02, 'b_in': jax.random.normal(ks[2], (3 * d,), dtype=jnp.float32) * 0.02, 'w_out': jax.random.normal(ks[3], (d, d), dtype=jnp.float32) * 0.02, 'b_out': jax.random.normal(ks[4], (d,), dtype=jnp.float32) * 0.02}
    _L0_attn_in = _L0_attn_setup()

    def _L0_ffn_setup():
        import jax, jax.numpy as jnp
        import numpy as np
        E = 8
        K = 2
        D = 128
        H = 342
        B, S = (2, 256)

        def _moe_forward(x, centroid, Wg, bg, W1, b1, W2, b2):
            T = x.shape[0] * x.shape[1]
            xs = x.reshape(T, D)
            d2 = jnp.sum(xs * xs, axis=-1, keepdims=True) + jnp.sum(centroid * centroid, axis=-1)[None, :] - 2.0 * (xs @ centroid.T)
            dist = jnp.sqrt(jnp.maximum(d2, 1e-12))
            w, sel = jax.lax.top_k(dist, K)
            w = jax.nn.softmax(w.astype(jnp.float32), axis=1).astype(x.dtype)
            we = jnp.zeros((T, E), dtype=x.dtype).at[jnp.arange(T)[:, None], sel].add(w)
            out = jnp.zeros_like(xs)
            for e in range(E):
                h = jax.nn.silu(xs @ Wg[e] + bg[e]) * (xs @ W1[e] + b1[e])
                out = out + we[:, e:e + 1] * (h @ W2[e] + b2[e])
            return out.reshape(x.shape)
        key = jax.random.key(seed)
        ks = jax.random.split(key, 9)
        scale = 0.02
        return {'x': jax.random.normal(ks[0], (B, S, D), dtype=jnp.float32), 'centroid': jax.random.normal(ks[1], (E, D), dtype=jnp.float32), 'Wg': jax.random.normal(ks[2], (E, D, H), dtype=jnp.float32) * scale, 'bg': jnp.zeros((E, H), dtype=jnp.float32), 'W1': jax.random.normal(ks[3], (E, D, H), dtype=jnp.float32) * scale, 'b1': jnp.zeros((E, H), dtype=jnp.float32), 'W2': jax.random.normal(ks[4], (E, H, D), dtype=jnp.float32) * scale, 'b2': jnp.zeros((E, D), dtype=jnp.float32)}
    _L0_ffn_in = _L0_ffn_setup()
    _d = {'L0_attn_x': _L0_attn_in['x'], 'L0_attn_w_in': _L0_attn_in['w_in'], 'L0_attn_b_in': _L0_attn_in['b_in'], 'L0_attn_w_out': _L0_attn_in['w_out'], 'L0_attn_b_out': _L0_attn_in['b_out'], 'L0_ffn_centroid': _L0_ffn_in['centroid'], 'L0_ffn_Wg': _L0_ffn_in['Wg'], 'L0_ffn_bg': _L0_ffn_in['bg'], 'L0_ffn_W1': _L0_ffn_in['W1'], 'L0_ffn_b1': _L0_ffn_in['b1'], 'L0_ffn_W2': _L0_ffn_in['W2'], 'L0_ffn_b2': _L0_ffn_in['b2']}
    _x0 = _d['L0_attn_x']
    _d['L0_attn_x'] = jax.random.normal(jax.random.fold_in(jax.random.key(seed), 1), (8, 256, 128), dtype=_x0.dtype)
    del _x0
    return _d

def reference(L0_attn_x, L0_attn_w_in, L0_attn_b_in, L0_attn_w_out, L0_attn_b_out, L0_ffn_centroid, L0_ffn_Wg, L0_ffn_bg, L0_ffn_W1, L0_ffn_b1, L0_ffn_W2, L0_ffn_b2):

    def _L0_attn_ref(x, w_in, b_in, w_out, b_out):
        import math
        import jax, jax.numpy as jnp
        import numpy as np
        N_HEADS = 16
        D_EMBED = 128
        b, l, d = x.shape
        h = N_HEADS
        scale = 1.0 / math.sqrt(d // h)
        x_proj = (x @ w_in.T + b_in).reshape(b, l, h, -1)
        q, k, v = jnp.split(x_proj, 3, axis=-1)
        att = jnp.einsum('blhd,bmhd->blmh', q, k) * scale
        att = jax.nn.softmax(att, axis=2)
        opt = jnp.einsum('blmh,blhd->blhd', att, v).reshape(b, l, d)
        return opt @ w_out.T + b_out

    def _L0_ffn_ref(x, centroid, Wg, bg, W1, b1, W2, b2):
        import jax, jax.numpy as jnp
        import numpy as np
        E = 8
        K = 2
        D = 128
        H = 342
        B, S = (2, 256)

        def _moe_forward(x, centroid, Wg, bg, W1, b1, W2, b2):
            T = x.shape[0] * x.shape[1]
            xs = x.reshape(T, D)
            d2 = jnp.sum(xs * xs, axis=-1, keepdims=True) + jnp.sum(centroid * centroid, axis=-1)[None, :] - 2.0 * (xs @ centroid.T)
            dist = jnp.sqrt(jnp.maximum(d2, 1e-12))
            w, sel = jax.lax.top_k(dist, K)
            w = jax.nn.softmax(w.astype(jnp.float32), axis=1).astype(x.dtype)
            we = jnp.zeros((T, E), dtype=x.dtype).at[jnp.arange(T)[:, None], sel].add(w)
            out = jnp.zeros_like(xs)
            for e in range(E):
                h = jax.nn.silu(xs @ Wg[e] + bg[e]) * (xs @ W1[e] + b1[e])
                out = out + we[:, e:e + 1] * (h @ W2[e] + b2[e])
            return out.reshape(x.shape)
        return _moe_forward(x, centroid, Wg, bg, W1, b1, W2, b2)
    x = L0_attn_x
    x = x + _layernorm(_L0_attn_ref(_layernorm(x, axis=-1), L0_attn_w_in, L0_attn_b_in, L0_attn_w_out, L0_attn_b_out), axis=-1)
    x = x + _layernorm(_L0_ffn_ref(_layernorm(x, axis=-1), L0_ffn_centroid, L0_ffn_Wg, L0_ffn_bg, L0_ffn_W1, L0_ffn_b1, L0_ffn_W2, L0_ffn_b2), axis=-1)
    return x

_drawn_inputs = setup_inputs


def setup_inputs(seed=0):
    import zlib

    import numpy as np

    out = dict(_drawn_inputs(seed))
    spreads = {'L0_ffn_bg': (0.0, 0.293), 'L0_ffn_b1': (0.0, 0.282), 'L0_ffn_b2': (0.0, 0.1)}
    factors = {}
    for name, (base, spread) in spreads.items():
        noise = np.random.default_rng([zlib.crc32(name.encode()), seed]).standard_normal(out[name].shape)
        drawn = base * np.exp(spread * noise) if base else spread * noise
        out[name] = jnp.asarray(drawn.astype(out[name].dtype))
    for name, factor in factors.items():
        out[name] = (out[name] * factor).astype(out[name].dtype)
    return out
```

```python
import concourse.bass as bass
from concourse import mybir
from contextlib import ExitStack


def need(eng, sem, value):
    if isinstance(value, int) and value <= 0:
        return
    eng.wait_ge(sem, value)


def sandwich_layer(nc, x, w_qk, b_qk, w_v, b_v, w_o, b_o, cent, wg, bg, w1, b1, w2, b2, parts, head_rows,
                   ident_in, iota_in, out):
    fp32, fp32r, u32 = mybir.dt.float32, mybir.dt.float32r, mybir.dt.uint32
    ALU, ACT, AX = mybir.AluOpType, mybir.ActivationFunctionType, mybir.AxisListType

    NB, L, D = x.shape
    T = L // 128
    E, _, H = wg.shape
    HC = 3
    HP = H // HC
    NH = 16
    HD = D // NH
    G = 4
    SG = T * G
    QK = 2 * G
    SCALE = float(HD) ** -0.5
    EPS = 1e-5
    LAST = NB - 1

    ctx = ExitStack()
    with ctx:
        def sb(name, shape, dt=fp32):
            return ctx.enter_context(nc.sbuf_tensor(name, shape, dt))

        def sem(name):
            return ctx.enter_context(nc.semaphore(name))

        ident = sb("ident", [128, 128])
        iota = sb("iota", [128, T, E])
        part_sel = sb("part_sel", [128, 4])
        head_sel = sb("head_sel", [128, 4])
        wqk_sb = sb("wqk_sb", [128, QK, 128])
        bqk_raw = sb("bqk_raw", [128, QK])
        bqk_sb = sb("bqk_sb", [128, QK])
        wv_sb = sb("wv_sb", [128, D])
        bv_sb = sb("bv_sb", [128, D])
        wo_sb = sb("wo_sb", [128, D])
        bo_sb = sb("bo_sb", [128, D])
        cent_sb = sb("cent_sb", [128, E])
        cent_sq = sb("cent_sq", [128, E])
        ones = sb("ones", [128, 128])
        cent_norm = sb("cent_norm", [128, T, E])
        w_raw = [sb(f"w_raw{i}", [128, E, H]) for i in range(2)]
        w_hi = [sb(f"w_hi{i}", [128, E, H], fp32r) for i in range(2)]
        w_lo = [sb(f"w_lo{i}", [128, E, H], fp32r) for i in range(2)]
        bg_sb = sb("bg_sb", [HP, E, HC])
        b1_sb = sb("b1_sb", [HP, E, HC])
        w2_sb = sb("w2_sb", [HP + 1, E, HC, D])
        half_pow = sb("half_pow", [128, T, E])
        rsqrt_pow = sb("rsqrt_pow", [128, T])

        x_sb = sb("x_sb", [128, 2, T, D])
        xn = sb("xn", [128, T, D])
        xnT = sb("xnT", [128, L])
        y_qk = sb("y_qk", [128, QK, L])
        y_sign = sb("y_sign", [128, QK, L], fp32r)
        qk_part = sb("qk_part", [128, QK, L], fp32r)
        q_head = sb("q_head", [128, G, 4, L], fp32r)
        v_sb = sb("v_sb", [128, T, D])
        neg_max = sb("neg_max", [128, SG, 4])
        row_sum = sb("row_sum", [128, T * NH])
        rec_sum = sb("rec_sum", [128, T * NH])
        att_w = sb("att_w", [128, T * NH])
        opt = sb("opt", [128, T, D])
        optT = sb("optT", [128, L])
        attn = sb("attn", [128, T, D])
        attn_n = sb("attn_n", [128, T, D])
        x1 = sb("x1", [128, 2, T, D])
        x2 = sb("x2", [128, T, D])
        x2_junk = sb("x2_junk", [128, T, D])
        x2_norm = sb("x2_norm", [128, T])
        x2T = sb("x2T", [128, L])
        x2_hi = sb("x2_hi", [128, L], fp32r)
        x2_lo = sb("x2_lo", [128, L], fp32r)
        dot_d = sb("dot_d", [128, T, E])
        dist_sum = sb("dist_sum", [128, T, E])
        dist_sq = sb("dist_sq", [128, T, E])
        dist = sb("dist", [128, T, E])
        top = sb("top", [128, T, 8])
        top_idx = sb("top_idx", [128, T, 8], u32)
        top_idf = sb("top_idf", [128, T, 2])
        pick = sb("pick", [128, 2, 2, T, E])
        delta = sb("delta", [128, 2, T])
        e_delta = sb("e_delta", [128, T])
        den = sb("den", [128, T])
        w_top = sb("w_top", [128, 2, T])
        w_pick = sb("w_pick", [128, 2, T, E])
        we = sb("we", [128, E, T])
        silu = sb("silu", [HP, 2, HC, L])
        h_sb = sb("h_sb", [128, E, HC, L])
        y_w = sb("y_w", [128, 2, 2, T, D])
        acc = sb("acc", [128, T * D])
        acc_n = sb("acc_n", [128, T, D])
        spare = sb("spare", [128, 1])
        out_sb = sb("out_sb", [128, 2, T, D])
        stats = {k: sb(f"stats_{k}", [128, T, 6]) for k in ("in", "attn", "mid", "moe")}
        mean_var = {k: sb(f"mean_var_{k}", [128, T, 2]) for k in ("in", "attn", "mid", "moe")}
        var_eps = {k: sb(f"var_eps_{k}", [128, T]) for k in ("in", "attn", "mid", "moe")}
        rstd = {k: sb(f"rstd_{k}", [128, T]) for k in ("in", "attn", "mid", "moe")}

        psum = ctx.enter_context(nc.psum_tensor("psum", [128, 8, 512], fp32))
        misc = [psum[:, 6, :], psum[:, 7, :]]

        def gu_bank(e):
            return psum[:, 3 * (e % 2):3 * (e % 2) + 3, :].rearrange("p a b -> p (a b)")

        def score_bank(g):
            return psum[:, 2 * (g % 2):2 * (g % 2) + 2, :].rearrange("p a b -> p (a b)")

        def y_bank(pair):
            return psum[:, 4 + pair % 2, :]

        consts_in = sem("consts_in")
        proj_w_in = sem("proj_w_in")
        moe_w_in = sem("moe_w_in")
        moe_w2_in = sem("moe_w2_in")
        x_in = [sem("x_in0"), sem("x_in1")]
        out_sent = [sem("out_sent0"), sem("out_sent1")]
        fills = sem("fills")
        bqk_scaled = sem("bqk_scaled")
        cent_sq_done = sem("cent_sq_done")
        cent_ps_ready = sem("cent_ps_ready")
        cent_norm_done = sem("cent_norm_done")
        w_hi_done = sem("w_hi_done")
        w_lo_done = sem("w_lo_done")
        ln_step = {k: sem(f"ln_step_{k}") for k in ("in", "attn", "mid", "moe")}
        ln_rstd = {k: sem(f"ln_rstd_{k}") for k in ("in", "attn", "mid", "moe")}
        xn_ready = sem("xn_ready")
        xnT_ps = sem("xnT_ps")
        xnT_ready = sem("xnT_ready")
        qk_ps = sem("qk_ps")
        qk_read = sem("qk_read")
        sign_ready = sem("sign_ready")
        part_ready = sem("part_ready")
        q_head_ready = sem("q_head_ready")
        v_ps = sem("v_ps")
        v_ready = sem("v_ready")
        scores_ready = sem("scores_ready")
        max_ready = sem("max_ready")
        exp_done = sem("exp_done")
        rec_done = sem("rec_done")
        att_w_done = sem("att_w_done")
        opt_ready = sem("opt_ready")
        optT_ps = sem("optT_ps")
        optT_ready = sem("optT_ready")
        attn_ps = sem("attn_ps")
        attn_ready = sem("attn_ready")
        attn_n_ready = sem("attn_n_ready")
        x1_ready = sem("x1_ready")
        x2_ready = sem("x2_ready")
        x2_norm_done = sem("x2_norm_done")
        x2T_ps = sem("x2T_ps")
        x2T_ready = sem("x2T_ready")
        x2_hi_ready = sem("x2_hi_ready")
        x2_lo_ready = sem("x2_lo_ready")
        dot_ps = sem("dot_ps")
        dot_read = sem("dot_read")
        dist_step = sem("dist_step")
        dist_sq_ready = sem("dist_sq_ready")
        dist_ready = sem("dist_ready")
        route_step = sem("route_step")
        delta_ready = sem("delta_ready")
        pick_ready = sem("pick_ready")
        e_delta_ready = sem("e_delta_ready")
        we_step = sem("we_step")
        we_ready = sem("we_ready")
        gu_ps = sem("gu_ps")
        silu_done = sem("silu_done")
        h_ready = sem("h_ready")
        y_ps = sem("y_ps")
        y_w_ready = sem("y_w_ready")
        acc_step = sem("acc_step")
        acc_n_ready = sem("acc_n_ready")
        out_ready = sem("out_ready")

        N_CONST, N_PROJ, N_MOE, N_W2 = 4 * 16, 7 * 16, 4 * 16, 2 * 16

        block = ctx.enter_context(nc.Block())

        def stages(eng, stage):
            stage(0, 0)
            stage(1, 1)
            with eng.Fori(1, NB // 2 - 1) as r:
                stage(2 * r, 0)
                stage(2 * r + 1, 1)
            for s in range(NB - 2, NB + 2):
                stage(s, s % 2)

        def kind(s):
            if not isinstance(s, int):
                return True, True, True
            return s < NB, 1 <= s <= NB, s >= 2

        @block.sync
        def _(sp):
            sp.dma_start(x_sb[:, 0, :, :], x[0].rearrange("(t p) d -> p t d", p=128)).then_inc(x_in[0], 16)
            sp.dma_start(ident[:, :], ident_in).then_inc(consts_in, 16)
            sp.dma_start(part_sel[:, :], parts).then_inc(consts_in, 16)
            sp.dma_start(head_sel[:, :], head_rows).then_inc(consts_in, 16)
            sp.dma_start(wqk_sb[:, :, :], w_qk).then_inc(proj_w_in, 16)
            sp.dma_start(bqk_raw[:, :], b_qk).then_inc(proj_w_in, 16)
            sp.dma_start(wv_sb[:, :], w_v).then_inc(proj_w_in, 16)
            sp.dma_start(bv_sb[:, :], b_v).then_inc(proj_w_in, 16)
            sp.dma_start(x_sb[:, 1, :, :], x[1].rearrange("(t p) d -> p t d", p=128)).then_inc(x_in[1], 16)
            sp.dma_start(wo_sb[:, :], w_o).then_inc(proj_w_in, 16)
            sp.dma_start(bo_sb[:, :], b_o).then_inc(proj_w_in, 16)
            sp.dma_start(cent_sb[:, :], cent).then_inc(proj_w_in, 16)
            sp.dma_start(iota[:, :, :], iota_in).then_inc(consts_in, 16)
            sp.dma_start(w_raw[0][:, :, :], wg.rearrange("e d h -> d e h")).then_inc(moe_w_in, 16)
            sp.dma_start(w_raw[1][:, :, :], w1.rearrange("e d h -> d e h")).then_inc(moe_w_in, 16)
            sp.dma_start(bg_sb[:, :, :], bg).then_inc(moe_w_in, 16)
            sp.dma_start(b1_sb[:, :, :], b1).then_inc(moe_w_in, 16)
            sp.dma_start(w2_sb[0:HP, :, :, :], w2.rearrange("e (c p) d -> p e c d", p=HP)).then_inc(moe_w2_in, 16)
            sp.dma_start(w2_sb[HP:HP + 1, :, 0, :], b2.rearrange("(a e) d -> a e d", a=1)).then_inc(moe_w2_in, 16)

            def load(b, par):
                need(sp, x1_ready, b - 1)
                sp.dma_start(x_sb[:, par, :, :],
                             x[bass.ds(b, 1), :, :].rearrange("b (t p) d -> p (b t) d", p=128)).then_inc(x_in[par], 16)

            def store(b, par):
                need(sp, out_ready, b + 1)
                sp.dma_start(out[bass.ds(b, 1), :, :].rearrange("b (t p) d -> p (b t) d", p=128),
                             out_sb[:, par, :, :]).then_inc(out_sent[par], 16)

            load(2, 0)
            with sp.Fori(1, NB // 2 - 1) as r:
                load(2 * r + 1, 1)
                store(2 * r - 2, 0)
                load(2 * r + 2, 0)
                store(2 * r - 1, 1)
            load(LAST, 1)
            for b in range(NB - 4, NB):
                store(b, b % 2)
            sp.wait_ge(out_sent[0], 16 * NB // 2)
            sp.wait_ge(out_sent[1], 16 * NB // 2)

        @block.tensor
        def _(pe):
            def transpose_rows(bank, rows, done):
                for t in range(T):
                    last = nc.tensor.transpose(bank[:, t * 128:(t + 1) * 128], rows[:, t, :], ident[:, :])
                last.then_inc(done, 1)

            def project_transpose(b):
                need(pe, xn_ready, b + 1)
                transpose_rows(misc[0], xn, xnT_ps)

            def project_qk(b, i):
                pe.wait_ge(qk_read, 8 * b + 2 * (i - 1)) if i >= 2 else None
                for n in range(2):
                    last = nc.tensor.matmul(misc[(i + 1) % 2][:, n * L:(n + 1) * L], wqk_sb[:, 2 * i + n, :],
                                            xnT[:, :], start=True, stop=True)
                last.then_inc(qk_ps, 1)

            def project_v(b):
                pe.wait_ge(qk_read, 8 * b + 8)
                for t in range(T):
                    last = nc.tensor.matmul(misc[0][:, t * D:(t + 1) * D], xnT[:, t * 128:(t + 1) * 128],
                                            wv_sb[:, :], start=True, stop=True)
                last.then_inc(v_ps, 1)

            def scores(s, gi):
                t, g = gi // G, gi % G
                if gi == 0:
                    pe.wait_ge(part_ready, 2 * s + 2)
                if t == 0:
                    pe.wait_ge(q_head_ready, G * s + g + 1)
                if gi < 2:
                    need(pe, h_ready, E * (s - 2) + E - 1 + gi)
                else:
                    pe.wait_ge(exp_done, SG * s + gi - 1)
                for j in range(4):
                    last = nc.tensor.matmul(score_bank(gi)[:, j * L:(j + 1) * L],
                                            q_head[:, g, j, t * 128:(t + 1) * 128], qk_part[:, G + g, :],
                                            start=True, stop=True)
                last.then_inc(scores_ready, 1)

            def second_product(b, e):
                if e == 0:
                    pe.wait_ge(h_ready, E * b + E)
                if e % 2 == 0 and e >= 4:
                    pe.wait_ge(y_w_ready, (E // 2) * b + e // 2 - 1)
                for t in range(T):
                    for c in range(HC):
                        k = HP + (c == 0)
                        last = nc.tensor.matmul(y_bank(e // 2)[:, ((e % 2) * T + t) * D:((e % 2) * T + t + 1) * D],
                                                h_sb[0:k, e, c, t * 128:(t + 1) * 128], w2_sb[0:k, e, c, :],
                                                start=(c == 0), stop=(c == HC - 1))
                if e % 2:
                    last.then_inc(y_ps, 1)

            def gate_up(b, e):
                if e == 0:
                    pe.wait_ge(x2_lo_ready, b + 1)
                    pe.wait_ge(exp_done, SG * NB if isinstance(b, int) and b == LAST else SG * (b + 2))
                elif e == 1:
                    need(pe, y_w_ready, (E // 2) * b)
                if e >= 2:
                    pe.wait_ge(h_ready, E * b + e - 1)
                bank = gu_bank(e)
                for c in range(HC):
                    for m in range(2):
                        hi = w_hi[m][:, e, c * HP:(c + 1) * HP]
                        lo = w_lo[m][:, e, c * HP:(c + 1) * HP]
                        dst = bank[0:HP, (m * HC + c) * L:(m * HC + c + 1) * L]
                        nc.tensor.matmul(dst, hi, x2_hi[:, :], start=True, stop=False)
                        nc.tensor.matmul(dst, hi, x2_lo[:, :], start=False, stop=False)
                        last = nc.tensor.matmul(dst, lo, x2_hi[:, :], start=False, stop=True)
                last.then_inc(gu_ps, 1)

            def stage(s, par):
                has_scores, has_gu, has_y = kind(s)
                has_proj = not isinstance(s, int) or s < LAST
                for gi in range(SG):
                    if has_scores:
                        scores(s, gi)
                    if has_y:
                        second_product(s - 2, gi)
                    if has_gu and gi == 1:
                        pe.wait_ge(x2_ready, s)
                        if has_scores:
                            pe.wait_ge(v_ready, s + 1)
                        transpose_rows(misc[0], x2, x2T_ps)
                    if has_gu and gi == 3:
                        pe.wait_ge(x2T_ready, s)
                        for t in range(T):
                            last = nc.tensor.matmul(misc[1][:, t * E:(t + 1) * E], x2T[:, t * 128:(t + 1) * 128],
                                                    cent_sb[:, :], start=True, stop=True)
                        last.then_inc(dot_ps, 1)
                if isinstance(s, int) and s == 1:
                    pe.wait_ge(w_lo_done, 2)
                    pe.wait_ge(moe_w2_in, N_W2)
                if has_proj:
                    need(pe, x2T_ready, s)
                    if isinstance(s, int) and s == 0:
                        pe.wait_ge(v_ready, 1)
                    project_transpose(s + 1)
                for e in range(E):
                    if has_gu:
                        gate_up(s - 1, e)
                    if e == 0 and has_proj:
                        pe.wait_ge(xnT_ready, s + 2)
                        need(pe, dot_read, s)
                        project_qk(s + 1, 0)
                        project_qk(s + 1, 1)
                    if e == 1 and has_proj:
                        project_qk(s + 1, 2)
                    if e == 2 and has_proj:
                        project_qk(s + 1, 3)
                    if e == 2 and has_scores:
                        if has_proj:
                            pe.wait_ge(qk_read, 8 * (s + 1) + 6)
                        else:
                            pe.wait_ge(dot_read, s)
                        pe.wait_ge(opt_ready, s + 1)
                        transpose_rows(misc[1], opt, optT_ps)
                    if e == 3 and has_proj:
                        project_v(s + 1)
                    if e == 4 and has_scores:
                        pe.wait_ge(optT_ready, s + 1)
                        for t in range(T):
                            last = nc.tensor.matmul(misc[1][:, t * D:(t + 1) * D], optT[:, t * 128:(t + 1) * 128],
                                                    wo_sb[:, :], start=True, stop=True)
                        last.then_inc(attn_ps, 1)

            pe.wait_ge(consts_in, N_CONST)
            pe.wait_ge(proj_w_in, N_PROJ)
            project_transpose(0)
            pe.wait_ge(cent_sq_done, 1)
            pe.wait_ge(fills, 4)
            nc.tensor.matmul(misc[1][:, 0:E], ones[:, :], cent_sq[:, :], start=True, stop=True).then_inc(cent_ps_ready, 1)
            pe.wait_ge(xnT_ready, 1)
            pe.wait_ge(cent_norm_done, 2)
            for i in range(QK // 2):
                project_qk(0, i)
            project_v(0)
            stages(pe, stage)

        @block.scalar
        def _(act):
            def evacuate_xnT(b):
                act.wait_ge(xnT_ps, b + 1)
                need(act, v_ps, b)
                nc.scalar.activation(xnT[:, :], misc[0][:, 0:L], ACT.Copy).then_inc(xnT_ready, 1)

            def evacuate_qk(b, i):
                act.wait_ge(qk_ps, 4 * b + i + 1)
                if i == 0:
                    need(act, part_ready, 2 * b)
                for n in range(2):
                    g = 2 * i + n
                    nc.scalar.activation(y_qk[:, g, :], misc[(i + 1) % 2][:, n * L:(n + 1) * L], ACT.Identity,
                                         bias=bqk_sb[:, g:g + 1], scale=SCALE if g < G else 1.0).then_inc(qk_read, 1)

            def exps(s, gi):
                act.wait_ge(max_ready, SG * s + gi + 1)
                if gi == 0:
                    need(act, att_w_done, s)
                for j in range(4):
                    tile = score_bank(gi)[:, j * L:(j + 1) * L]
                    last = nc.scalar.activation(tile, tile, ACT.Exp, bias=neg_max[:, gi, j:j + 1],
                                                accum_out=row_sum[:, gi * 4 + j:gi * 4 + j + 1])
                last.then_inc(exp_done, 1)

            def gate_silu(b, e):
                act.wait_ge(gu_ps, E * b + e + 1)
                if e >= 2:
                    act.wait_ge(h_ready, E * b + e - 1)
                else:
                    need(act, h_ready, E * b + e - 1)
                for c in range(HC):
                    last = nc.scalar.activation(silu[:, e % 2, c, :], gu_bank(e)[0:HP, c * L:(c + 1) * L], ACT.Silu,
                                                bias=bg_sb[:, e, c:c + 1])
                last.then_inc(silu_done, 1)

            def stage(s, par):
                has_scores, has_gu, has_y = kind(s)
                has_proj = not isinstance(s, int) or s < LAST
                if has_y:
                    act.wait_ge(delta_ready, s - 1)
                    need(act, we_step, 4 * (s - 2))
                    nc.scalar.activation(e_delta[:, :], delta[:, par, :], ACT.Exp).then_inc(e_delta_ready, 1)
                for gi in range(SG):
                    if has_scores:
                        exps(s, gi)
                    if has_gu and gi == 2:
                        act.wait_ge(x2T_ps, s)
                        need(act, dot_ps, s - 1)
                        need(act, x2_lo_ready, s - 1)
                        nc.scalar.activation(x2T[:, :], misc[0][:, 0:L], ACT.Copy).then_inc(x2T_ready, 1)
                if has_proj:
                    evacuate_xnT(s + 1)
                for e in range(E):
                    if has_gu:
                        gate_silu(s - 1, e)
                    if e == 0 and has_proj:
                        evacuate_qk(s + 1, 0)
                        evacuate_qk(s + 1, 1)
                    if e == 1 and has_proj:
                        evacuate_qk(s + 1, 2)
                    if e == 2 and has_proj:
                        evacuate_qk(s + 1, 3)
                    if e == 3 and has_scores:
                        act.wait_ge(optT_ps, s + 1)
                        need(act, attn_ps, s)
                        nc.scalar.activation(optT[:, :], misc[1][:, 0:L], ACT.Copy).then_inc(optT_ready, 1)

            evacuate_xnT(0)
            act.wait_ge(bqk_scaled, 2)
            for i in range(QK // 2):
                evacuate_qk(0, i)
            act.wait_ge(moe_w_in, N_MOE)
            stages(act, stage)

        @block.vector
        def _(dve):
            def ln_stats(k, src, b):
                step, n = ln_step[k], 5
                for t in range(T):
                    nc.vector.bn_stats(stats[k][:, t, :], src[:, t, :]).then_inc(step, 1)
                dve.wait_ge(step, n * b + 2)
                nc.vector.memset(spare[:, :], 0.0)
                for t in range(T):
                    nc.vector.bn_aggr(mean_var[k][:, t, :], stats[k][:, t, :]).then_inc(step, 1)
                dve.wait_ge(step, n * b + 4)
                nc.vector.tensor_scalar(var_eps[k][:, :], mean_var[k][:, :, 1], EPS, None, ALU.add).then_inc(step, 1)

            def ln_scale(k, dst, src, b, done):
                dve.wait_ge(ln_rstd[k], b + 1)
                for t in range(T):
                    last = nc.vector.tensor_scalar(dst[:, t, :], src[:, t, :], mean_var[k][:, t, 0:1],
                                                   rstd[k][:, t:t + 1], ALU.subtract, ALU.mult)
                last.then_inc(done, 1)

            def norm_input_stats(b, par):
                dve.wait_ge(x_in[par], 16 * ((b - par) // 2 + 1) if isinstance(b, int) else (b - par) * 8 + 16)
                ln_stats("in", x_sb[:, par, :, :], b)

            def norm_input(b, par):
                need(dve, xnT_ps, b)
                ln_scale("in", xn, x_sb[:, par, :, :], b, xn_ready)

            def split_qk(b, side):
                dve.wait_ge(qk_read, 8 * b + 4 * (side + 1))
                grp = slice(G * side, G * side + G)
                if side:
                    need(dve, scores_ready, SG * b)
                else:
                    need(dve, q_head_ready, G * b)
                nc.vector.tensor_scalar(y_sign[:, grp, :], y_qk[:, grp, :], part_sel[:, 2 * side + 1:2 * side + 2],
                                        None, ALU.mult).then_inc(sign_ready, 1)
                dve.wait_ge(sign_ready, 2 * b + side + 1)
                nc.vector.scalar_tensor_tensor(qk_part[:, grp, :], y_qk[:, grp, :], part_sel[:, 2 * side:2 * side + 1],
                                               y_sign[:, grp, :].bitcast(fp32), ALU.mult, ALU.add).then_inc(part_ready, 1)

            def take_v(b):
                dve.wait_ge(v_ps, b + 1)
                need(dve, opt_ready, b)
                nc.vector.tensor_tensor(v_sb[:, :, :], misc[0][:, 0:T * D].rearrange("p (t d) -> p t d", t=T),
                                        bv_sb[:, :].unsqueeze(1).to_broadcast([128, T, D]), ALU.add).then_inc(v_ready, 1)

            def row_max(s, gi):
                dve.wait_ge(scores_ready, SG * s + gi + 1)
                nc.vector.tensor_reduce(neg_max[:, gi, :], score_bank(gi).rearrange("p (j m) -> p j m", j=4),
                                        AX.X, ALU.max, negate=True).then_inc(max_ready, 1)

            def weight_values(b):
                dve.wait_ge(exp_done, SG * (b + 1))
                nc.vector.reciprocal(rec_sum[:, :], row_sum[:, :]).then_inc(rec_done, 1)
                dve.wait_ge(rec_done, b + 1)
                nc.vector.tensor_tensor(att_w[:, :], row_sum[:, :], rec_sum[:, :], ALU.mult).then_inc(att_w_done, 1)
                dve.wait_ge(att_w_done, b + 1)
                dve.wait_ge(v_ready, b + 1)
                need(dve, optT_ps, b)
                nc.vector.tensor_tensor(opt[:, :, :].rearrange("p t (h d) -> p (t h) d", d=HD),
                                        v_sb[:, :, :].rearrange("p t (h d) -> p (t h) d", d=HD),
                                        att_w[:, :].unsqueeze(2).to_broadcast([128, T * NH, HD]),
                                        ALU.mult).then_inc(opt_ready, 1)

            def take_attn(b):
                dve.wait_ge(attn_ps, b + 1)
                nc.vector.tensor_tensor(attn[:, :, :], misc[1][:, 0:T * D].rearrange("p (t d) -> p t d", t=T),
                                        bo_sb[:, :].unsqueeze(1).to_broadcast([128, T, D]), ALU.add).then_inc(attn_ready, 1)
                dve.wait_ge(attn_ready, b + 1)
                ln_stats("attn", attn, b)

            def add_attn(b, par):
                ln_scale("attn", attn_n, attn, b, attn_n_ready)
                dve.wait_ge(attn_n_ready, b + 1)
                nc.vector.tensor_tensor(x1[:, par, :, :], x_sb[:, par, :, :], attn_n[:, :, :], ALU.add).then_inc(x1_ready, 1)
                dve.wait_ge(x1_ready, b + 1)
                ln_stats("mid", x1[:, par, :, :], b)

            def norm_mid(b, par):
                need(dve, x2T_ps, b)
                ln_scale("mid", x2, x1[:, par, :, :], b, x2_ready)
                dve.wait_ge(x2_ready, b + 1)
                need(dve, dist_step, 2 * b)
                for t in range(T):
                    last = nc.vector.scalar_tensor_tensor(x2_junk[:, t, :], x2[:, t, :], 1.0, x2[:, t, :],
                                                          ALU.mult, ALU.mult, accum_out=x2_norm[:, t:t + 1])
                last.then_inc(x2_norm_done, 1)

            def split_x2(b):
                dve.wait_ge(x2T_ready, b + 1)
                need(dve, gu_ps, E * b)
                nc.vector.tensor_copy(x2_hi[:, :], x2T[:, :]).then_inc(x2_hi_ready, 1)
                dve.wait_ge(x2_hi_ready, b + 1)
                nc.vector.tensor_tensor(x2_lo[:, :], x2T[:, :], x2_hi[:, :].bitcast(fp32), ALU.subtract)\
                    .then_inc(x2_lo_ready, 1)

            def square_distance(b):
                dve.wait_ge(dot_ps, b + 1)
                dve.wait_ge(x2_norm_done, b + 1)
                nc.vector.scalar_tensor_tensor(dot_d[:, :, :], misc[1][:, 0:T * E].rearrange("p (t e) -> p t e", t=T),
                                               -2.0, cent_norm[:, :, :], ALU.mult, ALU.add).then_inc(dot_read, 1)
                dve.wait_ge(dot_read, b + 1)
                nc.vector.tensor_tensor(dist_sum[:, :, :], dot_d[:, :, :],
                                        x2_norm[:, :].unsqueeze(2).to_broadcast([128, T, E]), ALU.add).then_inc(dist_step, 1)
                dve.wait_ge(dist_step, 2 * b + 1)
                nc.vector.tensor_scalar(dist_sq[:, :, :], dist_sum[:, :, :], 1e-12, None, ALU.max).then_inc(dist_step, 1)

            def route(b, par):
                dve.wait_ge(dist_ready, b + 1)
                nc.vector.memset(spare[:, :], 0.0)
                for t in range(T):
                    nc.vector.max(top[:, t, :], dist[:, t, :]).then_inc(route_step, 1)
                dve.wait_ge(route_step, 6 * b + 2)
                nc.vector.tensor_tensor(delta[:, par, :], top[:, :, 1], top[:, :, 0], ALU.subtract).then_inc(delta_ready, 1)
                for t in range(T):
                    nc.vector.max_index(top_idx[:, t, :], top[:, t, :], dist[:, t, :]).then_inc(route_step, 1)
                dve.wait_ge(route_step, 6 * b + 4)
                nc.vector.tensor_copy(top_idf[:, :, :], top_idx[:, :, 0:2]).then_inc(route_step, 1)
                dve.wait_ge(route_step, 6 * b + 5)
                for k in range(2):
                    last = nc.vector.tensor_tensor(pick[:, par, k, :, :], iota[:, :, :],
                                                   top_idf[:, :, k:k + 1].to_broadcast([128, T, E]), ALU.is_equal)
                last.then_inc(route_step, 1)

            def expert_weights(b, par):
                dve.wait_ge(e_delta_ready, b + 1)
                nc.vector.tensor_scalar(den[:, :], e_delta[:, :], 1.0, None, ALU.add).then_inc(we_step, 1)
                dve.wait_ge(we_step, 4 * b + 1)
                nc.vector.reciprocal(w_top[:, 0, :], den[:, :]).then_inc(we_step, 1)
                dve.wait_ge(we_step, 4 * b + 2)
                nc.vector.tensor_tensor(w_top[:, 1, :], e_delta[:, :], w_top[:, 0, :], ALU.mult).then_inc(we_step, 1)
                dve.wait_ge(we_step, 4 * b + 3)
                dve.wait_ge(route_step, 6 * b + 6)
                for k in range(2):
                    last = nc.vector.tensor_tensor(w_pick[:, k, :, :], pick[:, par, k, :, :],
                                                   w_top[:, k, :].unsqueeze(2).to_broadcast([128, T, E]), ALU.mult)
                last.then_inc(we_step, 1)
                dve.wait_ge(we_step, 4 * b + 4)
                nc.vector.tensor_tensor(we[:, :, :].rearrange("p e t -> p t e"), w_pick[:, 0, :, :], w_pick[:, 1, :, :], ALU.add).then_inc(we_ready, 1)

            def hidden(b, e):
                dve.wait_ge(silu_done, E * b + e + 1)
                if e == 0:
                    need(dve, y_ps, (E // 2) * b)
                for c in range(HC):
                    last = nc.vector.scalar_tensor_tensor(h_sb[0:HP, e, c, :],
                                                          gu_bank(e)[0:HP, (HC + c) * L:(HC + c + 1) * L],
                                                          b1_sb[:, e, c:c + 1], silu[:, e % 2, c, :], ALU.add, ALU.mult)
                last.then_inc(h_ready, 1)

            def weight_outputs(b, pair):
                dve.wait_ge(y_ps, (E // 2) * b + pair + 1)
                if pair == 0:
                    dve.wait_ge(we_ready, b + 1)
                need(dve, acc_step, (E - 1) * b + max(2 * pair - 3, 0))
                nc.vector.tensor_tensor(y_w[:, pair % 2, :, :, :].rearrange("p a t d -> p (a t) d"),
                                        y_bank(pair).rearrange("p (a d) -> p a d", d=D),
                                        we[:, 2 * pair:2 * pair + 2, :].rearrange("p a t -> p (a t)").unsqueeze(2)
                                        .to_broadcast([128, 2 * T, D]),
                                        ALU.mult).then_inc(y_w_ready, 1)

            def finish_stats(b):
                dve.wait_ge(acc_step, (E - 1) * (b + 1))
                ln_stats("moe", acc[:, :].rearrange("p (t d) -> p t d", t=T), b)

            def finish(b, par):
                need(dve, out_sent[par], (b - par) * 8)
                ln_scale("moe", acc_n, acc[:, :].rearrange("p (t d) -> p t d", t=T), b, acc_n_ready)
                dve.wait_ge(acc_n_ready, b + 1)
                nc.vector.tensor_tensor(out_sb[:, par, :, :], x1[:, par, :, :], acc_n[:, :, :], ALU.add)\
                    .then_inc(out_ready, 1)

            def stage(s, par):
                has_scores, has_gu, has_y = kind(s)
                has_proj = not isinstance(s, int) or s < LAST
                for gi in range(SG):
                    if has_scores:
                        row_max(s, gi)
                    if has_y and gi == 0:
                        expert_weights(s - 2, par)
                    if has_y and gi % 2 and gi >= 1:
                        weight_outputs(s - 2, gi // 2)
                    if has_gu and gi == 2:
                        split_x2(s - 1)
                    if has_gu and gi == 4:
                        square_distance(s - 1)
                    if has_proj and gi == 5:
                        norm_input_stats(s + 1, 1 - par)
                    if has_proj and gi == 6:
                        norm_input(s + 1, 1 - par)
                if has_scores:
                    weight_values(s)
                if isinstance(s, int) and s == 0:
                    split_weights()
                for e in range(E):
                    if has_gu:
                        hidden(s - 1, e)
                    if e == 0 and has_y:
                        finish_stats(s - 2)
                    if e == 1 and has_y:
                        finish(s - 2, par)
                    if e == 1 and has_proj:
                        split_qk(s + 1, 0)
                    if e == 2 and has_gu:
                        route(s - 1, 1 - par)
                    if e == 3 and has_proj:
                        split_qk(s + 1, 1)
                    if e == 4 and has_proj:
                        take_v(s + 1)
                    if e == 5 and has_scores:
                        take_attn(s)
                    if e == 6 and has_scores:
                        add_attn(s, par)
                    if e == 7 and has_scores:
                        norm_mid(s, par)

            def split_weights():
                dve.wait_ge(moe_w_in, N_MOE)
                for m in range(2):
                    nc.vector.tensor_copy(w_hi[m][:, :, :], w_raw[m][:, :, :]).then_inc(w_hi_done, 1)
                    dve.wait_ge(w_hi_done, m + 1)
                    nc.vector.tensor_tensor(w_lo[m][:, :, :], w_raw[m][:, :, :], w_hi[m][:, :, :].bitcast(fp32),
                                            ALU.subtract).then_inc(w_lo_done, 1)

            norm_input_stats(0, 0)
            norm_input(0, 0)
            dve.wait_ge(proj_w_in, N_PROJ)
            dve.wait_ge(consts_in, N_CONST)
            nc.vector.tensor_scalar(bqk_sb[:, 0:G], bqk_raw[:, 0:G], SCALE, None, ALU.mult).then_inc(bqk_scaled, 1)
            nc.vector.tensor_copy(bqk_sb[:, G:QK], bqk_raw[:, G:QK]).then_inc(bqk_scaled, 1)
            nc.vector.tensor_tensor(cent_sq[:, :], cent_sb[:, :], cent_sb[:, :], ALU.mult).then_inc(cent_sq_done, 1)
            dve.wait_ge(cent_ps_ready, 1)
            for t in range(T):
                nc.vector.tensor_copy(cent_norm[:, t, :], misc[1][:, 0:E]).then_inc(cent_norm_done, 1)
            split_qk(0, 0)
            split_qk(0, 1)
            take_v(0)
            stages(dve, stage)

        @block.gpsimd
        def _(pool):
            def ln_root(k, b):
                pool.wait_ge(ln_step[k], 5 * b + 5)
                nc.gpsimd.tensor_tensor(rstd[k][:, :], var_eps[k][:, :], rsqrt_pow[:, :], ALU.pow).then_inc(ln_rstd[k], 1)

            def mask_heads(b, g):
                pool.wait_ge(part_ready, 2 * b + 1)
                if g == 0:
                    need(pool, scores_ready, SG * b)
                nc.gpsimd.tensor_tensor(q_head[:, g, :, :],
                                        qk_part[:, g, :].bitcast(fp32).unsqueeze(1).to_broadcast([128, 4, L]),
                                        head_sel[:, :].unsqueeze(2).to_broadcast([128, 4, L]),
                                        ALU.mult).then_inc(q_head_ready, 1)

            def accumulate(b, pair):
                pool.wait_ge(y_w_ready, (E // 2) * b + pair + 1)
                ya = [y_w[:, pair % 2, a, :, :].rearrange("p t d -> p (t d)") for a in range(2)]
                if pair == 0:
                    need(pool, acc_n_ready, b)
                    nc.gpsimd.tensor_tensor(acc[:, :], ya[0], ya[1], ALU.add).then_inc(acc_step, 1)
                else:
                    for a in range(2):
                        pool.wait_ge(acc_step, (E - 1) * b + 2 * pair - 1 + a)
                        nc.gpsimd.tensor_tensor(acc[:, :], acc[:, :], ya[a], ALU.add).then_inc(acc_step, 1)

            def stage(s, par):
                has_scores, has_gu, has_y = kind(s)
                has_proj = not isinstance(s, int) or s < LAST
                for pair in range(E // 2):
                    if has_y:
                        accumulate(s - 2, pair)
                    if pair == 2 and has_gu:
                        pool.wait_ge(dist_step, 2 * s)
                        nc.gpsimd.tensor_tensor(dist[:, :, :], dist_sq[:, :, :], half_pow[:, :, :], ALU.pow)\
                            .then_inc(dist_ready, 1)
                    if pair == 2 and has_proj:
                        ln_root("in", s + 1)
                if has_y:
                    ln_root("moe", s - 2)
                if has_proj:
                    for g in range(G):
                        mask_heads(s + 1, g)
                if has_scores:
                    ln_root("attn", s)
                    ln_root("mid", s)

            nc.gpsimd.memset(rsqrt_pow[:, :], -0.5).then_inc(fills, 1)
            nc.gpsimd.memset(half_pow[:, :, :], 0.5).then_inc(fills, 1)
            nc.gpsimd.memset(ones[:, :], 1.0).then_inc(fills, 1)
            nc.gpsimd.memset(h_sb[:, :, 0, :], 1.0).then_inc(fills, 1)
            pool.wait_ge(fills, 2)
            ln_root("in", 0)
            pool.wait_ge(consts_in, N_CONST)
            for g in range(G):
                mask_heads(0, g)
            stages(pool, stage)


def kernel(L0_attn_x, L0_attn_w_in, L0_attn_b_in, L0_attn_w_out, L0_attn_b_out, L0_ffn_centroid, L0_ffn_Wg, L0_ffn_bg,
           L0_ffn_W1, L0_ffn_b1, L0_ffn_W2, L0_ffn_b2):
    import numpy as np
    import concourse.bacc as bacc
    from concourse.bass_utils import run_bass_kernel_spmd

    def arr(a):
        return np.ascontiguousarray(a)

    d, heads, experts = 128, 16, 8
    hd = d // heads
    w_in, b_in = arr(L0_attn_w_in), arr(L0_attn_b_in)
    rows = [[(4 * g + i) * 3 * hd + side * hd + k for i in range(4) for p in range(4) for k in range(hd)]
            for side in range(2) for g in range(heads // 4)]
    v_rows = [h * 3 * hd + 2 * hd + k for h in range(heads) for k in range(hd)]
    part = (np.arange(128) // hd) % 4
    lo = np.stack([part // 2, part % 2], 0)
    parts = np.stack([lo[0], 1 - 2 * lo[0], lo[1], 1 - 2 * lo[1]], 1).astype(np.float32)
    head_rows = (np.arange(128)[:, None] // 32 == np.arange(4)[None, :]).astype(np.float32)
    iota = np.tile(np.arange(experts, dtype=np.float32), (128, 2, 1))

    def chunks(bias):
        return arr(arr(bias).reshape(experts, 3, -1).transpose(2, 0, 1))

    arrays = {
        "x": arr(L0_attn_x),
        "w_qk": arr(w_in[np.array(rows)].transpose(2, 0, 1)),
        "b_qk": arr(b_in[np.array(rows)].T),
        "w_v": arr(w_in[np.array(v_rows)].T),
        "b_v": arr(np.tile(b_in[np.array(v_rows)], (128, 1))),
        "w_o": arr(arr(L0_attn_w_out).T),
        "b_o": arr(np.tile(arr(L0_attn_b_out), (128, 1))),
        "cent": arr(arr(L0_ffn_centroid).T),
        "wg": arr(L0_ffn_Wg), "bg": chunks(L0_ffn_bg), "w1": arr(L0_ffn_W1), "b1": chunks(L0_ffn_b1),
        "w2": arr(L0_ffn_W2), "b2": arr(L0_ffn_b2),
        "parts": parts, "head_rows": head_rows, "ident": np.eye(128, dtype=np.float32), "iota": iota,
    }
    nc = bacc.Bacc("TRN2", target_bir_lowering=False, num_devices=1)
    aps = [nc.dram_tensor(f"in_{n}", a.shape, mybir.dt.from_np(a.dtype), kind="ExternalInput").ap() for n, a in arrays.items()]
    out = nc.dram_tensor("out", arrays["x"].shape, mybir.dt.float32, kind="ExternalOutput").ap()
    sandwich_layer(nc, *aps, out)
    return run_bass_kernel_spmd(nc, [{f"in_{n}": a for n, a in arrays.items()}], core_ids=[0]).results[0]["out"]
```

```python
import concourse.bass as bass
from concourse import mybir
from contextlib import ExitStack


def need(eng, sem, value):
    if isinstance(value, int) and value <= 0:
        return
    eng.wait_ge(sem, value)


def sandwich_layer(nc, x, w_qk, b_qk, w_v, b_v, w_o, b_o, cent, wg, bg, w1, b1, w2, b2, parts, head_rows,
                   ident_in, iota_in, out):
    fp32, fp32r, u32 = mybir.dt.float32, mybir.dt.float32r, mybir.dt.uint32
    ALU, ACT, AX = mybir.AluOpType, mybir.ActivationFunctionType, mybir.AxisListType

    NB, L, D = x.shape
    T = L // 128
    E, _, H = wg.shape
    HC = 3
    HP = H // HC
    NH = 16
    HD = D // NH
    G = 4
    NU = NH * T // 2
    QK = 2 * G
    SCALE = float(HD) ** -0.5
    EPS = 1e-5
    LAST = NB - 1

    ctx = ExitStack()
    with ctx:
        def sb(name, shape, dt=fp32):
            return ctx.enter_context(nc.sbuf_tensor(name, shape, dt))

        def sem(name):
            return ctx.enter_context(nc.semaphore(name))

        ident = sb("ident", [128, 128])
        iota = sb("iota", [128, T, E])
        part_sel = sb("part_sel", [128, 4])
        head_sel = sb("head_sel", [128, 4])
        wqkv_raw = sb("wqkv_raw", [128, QK + 1, 128])
        wqkv_hi = sb("wqkv_hi", [128, QK + 1, 128], fp32r)
        wqkv_lo = sb("wqkv_lo", [128, QK + 1, 128], fp32r)
        bqk_raw = sb("bqk_raw", [128, QK])
        bqk_sb = sb("bqk_sb", [128, QK])
        bv_sb = sb("bv_sb", [128, D])
        wo_sb = sb("wo_sb", [128, D])
        bo_sb = sb("bo_sb", [128, D])
        cent_sb = sb("cent_sb", [128, E])
        cent_hi = sb("cent_hi", [128, E], fp32r)
        cent_lo = sb("cent_lo", [128, E], fp32r)
        cent_sq = sb("cent_sq", [128, E])
        ones = sb("ones", [128, 128])
        cent_norm = sb("cent_norm", [128, T, E])
        w_raw = [sb(f"w_raw{i}", [128, E, H]) for i in range(2)]
        w_hi = [sb(f"w_hi{i}", [128, E, H], fp32r) for i in range(2)]
        w_lo = [sb(f"w_lo{i}", [128, E, H], fp32r) for i in range(2)]
        bg_sb = sb("bg_sb", [HP, E, HC])
        b1_sb = sb("b1_sb", [HP, E, HC])
        w2_sb = sb("w2_sb", [HP + 1, E, HC, D])
        half_pow = sb("half_pow", [128, T, E])
        rsqrt_pow = sb("rsqrt_pow", [128, T])

        x_sb = sb("x_sb", [128, 2, T, D])
        xn = sb("xn", [128, T, D])
        xnT_hi = sb("xnT_hi", [128, L], fp32r)
        xnT_lo = sb("xnT_lo", [128, L], fp32r)
        y_qk = sb("y_qk", [128, QK, L])
        y_sign = sb("y_sign", [128, QK, L], fp32r)
        qk_part = sb("qk_part", [128, QK, L], fp32r)
        q_head = sb("q_head", [128, G, 4, L], fp32r)
        v_sb = sb("v_sb", [128, T, D])
        neg_max = sb("neg_max", [128, NU, 2])
        row_sum = sb("row_sum", [128, T * NH])
        rec_sum = sb("rec_sum", [128, T * NH])
        att_w = sb("att_w", [128, T * NH])
        opt = sb("opt", [128, T, D])
        optT = sb("optT", [128, L])
        attn = sb("attn", [128, T, D])
        attn_n = sb("attn_n", [128, T, D])
        x1 = sb("x1", [128, 2, T, D])
        x2 = sb("x2", [128, T, D])
        x2_junk = sb("x2_junk", [128, T, D])
        x2_norm = sb("x2_norm", [128, T])
        x2_hi = sb("x2_hi", [128, L], fp32r)
        x2_lo = sb("x2_lo", [128, L], fp32r)
        dot_d = sb("dot_d", [128, T, E])
        dist_sum = sb("dist_sum", [128, T, E])
        dist_sq = sb("dist_sq", [128, T, E])
        dist = sb("dist", [128, T, E])
        top = sb("top", [128, T, 8])
        top_idx = sb("top_idx", [128, T, 8], u32)
        top_idf = sb("top_idf", [128, T, 2])
        pick = sb("pick", [128, 2, 2, T, E])
        delta = sb("delta", [128, 2, T])
        e_delta = sb("e_delta", [128, T])
        den = sb("den", [128, T])
        w_top = sb("w_top", [128, 2, T])
        w_pick = sb("w_pick", [128, 2, T, E])
        we = sb("we", [128, E, T])
        silu = sb("silu", [HP, 2, HC, L])
        h_sb = sb("h_sb", [128, E, HC, L])
        y_w = sb("y_w", [128, 2, 2, T, D])
        acc = sb("acc", [128, T * D])
        acc_n = sb("acc_n", [128, T, D])
        spare = sb("spare", [128, 1])
        out_sb = sb("out_sb", [128, 2, T, D])
        stats = {k: sb(f"stats_{k}", [128, T, 6]) for k in ("in", "attn", "mid", "moe")}
        mean_var = {k: sb(f"mean_var_{k}", [128, T, 2]) for k in ("in", "attn", "mid", "moe")}
        var_eps = {k: sb(f"var_eps_{k}", [128, T]) for k in ("in", "attn", "mid", "moe")}
        rstd = {k: sb(f"rstd_{k}", [128, T]) for k in ("in", "attn", "mid", "moe")}

        psum = ctx.enter_context(nc.psum_tensor("psum", [128, 8, 512], fp32))
        misc = [psum[:, 6, :], psum[:, 7, :]]

        def gu_bank(e):
            return psum[:, 3 * (e % 2):3 * (e % 2) + 3, :].rearrange("p a b -> p (a b)")

        UP_AT = (4, 5, 3)

        def score_bank(u):
            return psum[:, (0, 1, 3, 4)[u % 4], :]

        def y_bank(pair):
            return psum[:, 2 + 3 * (pair % 2), :]

        consts_in = sem("consts_in")
        ident_in_sem = sem("ident_in_sem")
        qk_w_in = sem("qk_w_in")
        proj_w_in = sem("proj_w_in")
        w_raw_in = [sem("w_gate_in"), sem("w_up_in")]
        moe_b_in = sem("moe_b_in")
        moe_w2_in = sem("moe_w2_in")
        x_in = [sem("x_in0"), sem("x_in1")]
        out_sent = sem("out_sent")
        fills = sem("fills")
        bqk_scaled = sem("bqk_scaled")
        cent_sq_done = sem("cent_sq_done")
        cent_ps_ready = sem("cent_ps_ready")
        cent_norm_done = sem("cent_norm_done")
        w_hi_done = sem("w_hi_done")
        w_lo_done = sem("w_lo_done")
        ln_step = {k: sem(f"ln_step_{k}") for k in ("in", "attn", "mid", "moe")}
        ln_rstd = {k: sem(f"ln_rstd_{k}") for k in ("in", "attn", "mid", "moe")}
        xn_ready = sem("xn_ready")
        xnT_ps = sem("xnT_ps")
        xnT_hi_ready = sem("xnT_hi_ready")
        xnT_lo_ready = sem("xnT_lo_ready")
        wqkv_hi_done = sem("wqkv_hi_done")
        wqkv_lo_done = sem("wqkv_lo_done")
        cent_hi_done = sem("cent_hi_done")
        cent_lo_done = sem("cent_lo_done")
        qk_ps = sem("qk_ps")
        qk_read = sem("qk_read")
        sign_ready = sem("sign_ready")
        part_ready = sem("part_ready")
        q_head_ready = sem("q_head_ready")
        v_ps = sem("v_ps")
        v_ready = sem("v_ready")
        scores_ready = sem("scores_ready")
        max_ready = sem("max_ready")
        exp_done = sem("exp_done")
        rec_done = sem("rec_done")
        att_w_done = sem("att_w_done")
        opt_ready = sem("opt_ready")
        optT_ps = sem("optT_ps")
        optT_ready = sem("optT_ready")
        attn_ps = sem("attn_ps")
        attn_ready = sem("attn_ready")
        attn_n_ready = sem("attn_n_ready")
        x1_ready = sem("x1_ready")
        x2_ready = sem("x2_ready")
        x2_norm_done = sem("x2_norm_done")
        x2T_ps = sem("x2T_ps")
        x2_hi_ready = sem("x2_hi_ready")
        x2_lo_ready = sem("x2_lo_ready")
        dot_ps = sem("dot_ps")
        dot_read = sem("dot_read")
        dist_step = sem("dist_step")
        dist_sq_ready = sem("dist_sq_ready")
        dist_ready = sem("dist_ready")
        route_step = sem("route_step")
        delta_ready = sem("delta_ready")
        pick_ready = sem("pick_ready")
        e_delta_ready = sem("e_delta_ready")
        we_step = sem("we_step")
        we_ready = sem("we_ready")
        gu_ps = sem("gu_ps")
        silu_done = sem("silu_done")
        h_ready = sem("h_ready")
        y_ps = sem("y_ps")
        y_w_ready = sem("y_w_ready")
        acc_step = sem("acc_step")
        acc_n_ready = sem("acc_n_ready")
        out_ready = sem("out_ready")

        N_CONST, N_QK, N_PROJ, N_MOE, N_W2 = 3 * 16, 3 * 16, 4 * 16, 2 * 16, 2 * 16

        block = ctx.enter_context(nc.Block())

        def stages(eng, stage):
            stage(0, 0)
            stage(1, 1)
            with eng.Fori(1, NB // 2 - 1) as r:
                stage(2 * r, 0)
                stage(2 * r + 1, 1)
            for s in range(NB - 2, NB + 2):
                stage(s, s % 2)

        def kind(s):
            if not isinstance(s, int):
                return True, True, True
            return s < NB, 1 <= s <= NB, s >= 2

        @block.sync
        def _(sp):
            sp.dma_start(x_sb[:, 0, :, :], x[0].rearrange("(t p) d -> p t d", p=128)).then_inc(x_in[0], 16)
            sp.dma_start(ident[:, :], ident_in).then_inc(ident_in_sem, 16)
            sp.dma_start(wqkv_raw[:, 0:QK, :], w_qk).then_inc(qk_w_in, 16)
            sp.dma_start(wqkv_raw[:, QK, :], w_v).then_inc(qk_w_in, 16)
            sp.dma_start(bqk_raw[:, :], b_qk).then_inc(qk_w_in, 16)
            sp.dma_start(part_sel[:, :], parts).then_inc(consts_in, 16)
            sp.dma_start(head_sel[:, :], head_rows).then_inc(consts_in, 16)
            sp.dma_start(iota[:, :, :], iota_in).then_inc(consts_in, 16)
            sp.dma_start(bv_sb[:, :], b_v).then_inc(proj_w_in, 16)
            sp.dma_start(x_sb[:, 1, :, :], x[1].rearrange("(t p) d -> p t d", p=128)).then_inc(x_in[1], 16)
            sp.dma_start(wo_sb[:, :], w_o).then_inc(proj_w_in, 16)
            sp.dma_start(bo_sb[:, :], b_o).then_inc(proj_w_in, 16)
            sp.dma_start(cent_sb[:, :], cent).then_inc(proj_w_in, 16)
            sp.dma_start(w_raw[0][:, :, :], wg.rearrange("e d h -> d e h")).then_inc(w_raw_in[0], 16)
            sp.dma_start(w_raw[1][:, :, :], w1.rearrange("e d h -> d e h")).then_inc(w_raw_in[1], 16)
            sp.dma_start(bg_sb[:, :, :], bg).then_inc(moe_b_in, 16)
            sp.dma_start(b1_sb[:, :, :], b1).then_inc(moe_b_in, 16)
            sp.dma_start(w2_sb[0:HP, :, :, :], w2.rearrange("e (c p) d -> p e c d", p=HP)).then_inc(moe_w2_in, 16)
            sp.dma_start(w2_sb[HP:HP + 1, :, 0, :], b2.rearrange("(a e) d -> a e d", a=1)).then_inc(moe_w2_in, 16)

            def load(b, par):
                need(sp, x1_ready, b - 1)
                sp.dma_start(x_sb[:, par, :, :],
                             x[bass.ds(b, 1), :, :].rearrange("b (t p) d -> p (b t) d", p=128)).then_inc(x_in[par], 16)

            def store(b, par):
                need(sp, out_ready, b + 1)
                sp.dma_start(out[bass.ds(b, 1), :, :].rearrange("b (t p) d -> p (b t) d", p=128),
                             out_sb[:, par, :, :]).then_inc(out_sent, 16)

            load(2, 0)
            with sp.Fori(1, NB // 2 - 1) as r:
                load(2 * r + 1, 1)
                store(2 * r - 2, 0)
                sp.wait_ge(out_sent, 16 * (2 * r - 1))
                load(2 * r + 2, 0)
                store(2 * r - 1, 1)
            load(LAST, 1)
            for b in range(NB - 4, NB):
                store(b, b % 2)
            sp.wait_ge(out_sent, 16 * NB)

        @block.tensor
        def _(pe):
            def transpose_rows(bank, rows, done):
                for t in range(T):
                    last = nc.tensor.transpose(bank[:, t * 128:(t + 1) * 128], rows[:, t, :], ident[:, :])
                last.then_inc(done, 1)

            def product(dst, sta_hi, sta_lo, mov_hi, mov_lo):
                nc.tensor.matmul(dst, sta_hi, mov_hi, start=True, stop=False)
                nc.tensor.matmul(dst, sta_hi, mov_lo, start=False, stop=False)
                return nc.tensor.matmul(dst, sta_lo, mov_hi, start=False, stop=True)

            def project_transpose(b):
                need(pe, xn_ready, b + 1)
                transpose_rows(misc[0], xn, xnT_ps)

            def project_qk(b, i):
                pe.wait_ge(qk_read, 8 * b + 2 * (i - 1)) if i >= 2 else None
                for n in range(2):
                    last = product(misc[(i + 1) % 2][:, n * L:(n + 1) * L], wqkv_hi[:, 2 * i + n, :],
                                   wqkv_lo[:, 2 * i + n, :], xnT_hi[:, :], xnT_lo[:, :])
                last.then_inc(qk_ps, 1)

            def project_v(b):
                pe.wait_ge(qk_read, 8 * b + 8)
                for t in range(T):
                    rows = slice(t * 128, (t + 1) * 128)
                    last = product(misc[0][:, t * D:(t + 1) * D], xnT_hi[:, rows], xnT_lo[:, rows],
                                   wqkv_hi[:, QK, :], wqkv_lo[:, QK, :])
                last.then_inc(v_ps, 1)

            def scores(s, u):
                t, g, half = u // (2 * G), u // 2 % G, u % 2
                if u == 0:
                    pe.wait_ge(part_ready, 2 * s + 2)
                if t == 0 and half == 0:
                    pe.wait_ge(q_head_ready, G * s + g + 1)
                if u < 4:
                    need(pe, h_ready, E * (s - 2) + E - 1 + u // 2)
                else:
                    pe.wait_ge(exp_done, NU * s + u - 3)
                for n in range(2):
                    last = nc.tensor.matmul(score_bank(u)[:, n * L:(n + 1) * L],
                                            q_head[:, g, 2 * half + n, t * 128:(t + 1) * 128], qk_part[:, G + g, :],
                                            start=True, stop=True)
                last.then_inc(scores_ready, 1)

            def second_product(b, e):
                if e == 0:
                    pe.wait_ge(h_ready, E * b + E - 1)
                elif e == 2:
                    pe.wait_ge(h_ready, E * b + E)
                if e % 2 == 0 and e >= 4:
                    pe.wait_ge(y_w_ready, (E // 2) * b + e // 2 - 1)
                for t in range(T):
                    for c in range(HC):
                        k = HP + (c == 0)
                        last = nc.tensor.matmul(y_bank(e // 2)[:, ((e % 2) * T + t) * D:((e % 2) * T + t + 1) * D],
                                                h_sb[0:k, e, c, t * 128:(t + 1) * 128], w2_sb[0:k, e, c, :],
                                                start=(c == 0), stop=(c == HC - 1))
                if e % 2:
                    last.then_inc(y_ps, 1)

            def gate_up(b, e):
                if e < 2:
                    pe.wait_ge(exp_done, NU * (LAST + 1) if isinstance(b, int) and b == LAST
                               else NU * (b + 2) - 2 + 2 * e)
                    need(pe, y_w_ready, (E // 2) * b - 1 + e)
                if e == 0:
                    pe.wait_ge(x2_lo_ready, b + 1)
                if e >= 2:
                    pe.wait_ge(h_ready, E * b + e - 1)
                bank = gu_bank(e)
                for c in range(HC):
                    for m in range(2):
                        hi = w_hi[m][:, e, c * HP:(c + 1) * HP]
                        lo = w_lo[m][:, e, c * HP:(c + 1) * HP]
                        at = UP_AT[c] if m else c
                        dst = bank[0:HP, at * L:(at + 1) * L]
                        last = product(dst, hi, lo, x2_hi[:, :], x2_lo[:, :])
                last.then_inc(gu_ps, 1)

            def stage(s, par):
                has_scores, has_gu, has_y = kind(s)
                has_proj = not isinstance(s, int) or s < LAST
                if has_scores:
                    scores(s, 0)
                    scores(s, 1)
                for e in range(E):
                    if has_y:
                        second_product(s - 2, e)
                    if has_scores:
                        for u in {0: (2, 3, 4), 1: (5, 6)}.get(e, (2 * e + 3, 2 * e + 4)):
                            if u < NU:
                                scores(s, u)
                    if has_gu and e == 2:
                        pe.wait_ge(x2_ready, s)
                        if has_scores:
                            pe.wait_ge(v_ready, s + 1)
                        transpose_rows(misc[0], x2, x2T_ps)
                    if has_gu and e == 5:
                        pe.wait_ge(x2_lo_ready, s)
                        for t in range(T):
                            rows = slice(t * 128, (t + 1) * 128)
                            last = product(misc[1][:, t * E:(t + 1) * E], x2_hi[:, rows], x2_lo[:, rows],
                                           cent_hi[:, :], cent_lo[:, :])
                        last.then_inc(dot_ps, 1)
                    if has_proj and e == 6:
                        need(pe, x2_lo_ready, s)
                        if isinstance(s, int) and s == 0:
                            pe.wait_ge(v_ready, 1)
                        project_transpose(s + 1)
                if has_proj:
                    need(pe, dot_read, s)
                    pe.wait_ge(xnT_lo_ready, s + 2)
                    project_qk(s + 1, 0)
                    project_qk(s + 1, 1)
                if isinstance(s, int) and s == 1:
                    pe.wait_ge(w_lo_done, 2 * E)
                    pe.wait_ge(moe_w2_in, N_W2)
                for e in range(E):
                    if has_gu:
                        gate_up(s - 1, e)
                    if e == 0 and has_proj:
                        project_qk(s + 1, 2)
                    if e == 1 and has_proj:
                        project_qk(s + 1, 3)
                    if e == 2 and has_scores:
                        if has_proj:
                            pe.wait_ge(qk_read, 8 * (s + 1) + 6)
                        else:
                            pe.wait_ge(dot_read, s)
                        pe.wait_ge(opt_ready, s + 1)
                        transpose_rows(misc[1], opt, optT_ps)
                    if e == 3 and has_proj:
                        project_v(s + 1)
                    if e == 4 and has_scores:
                        pe.wait_ge(optT_ready, s + 1)
                        for t in range(T):
                            last = nc.tensor.matmul(misc[1][:, t * D:(t + 1) * D], optT[:, t * 128:(t + 1) * 128],
                                                    wo_sb[:, :], start=True, stop=True)
                        last.then_inc(attn_ps, 1)

            pe.wait_ge(ident_in_sem, 16)
            project_transpose(0)
            pe.wait_ge(xnT_lo_ready, 1)
            pe.wait_ge(wqkv_lo_done, 2)
            for i in range(QK // 2):
                project_qk(0, i)
            project_v(0)
            pe.wait_ge(proj_w_in, N_PROJ)
            pe.wait_ge(cent_lo_done, 1)
            pe.wait_ge(cent_sq_done, 1)
            pe.wait_ge(fills, 4)
            nc.tensor.matmul(misc[1][:, 0:E], ones[:, :], cent_sq[:, :], start=True, stop=True).then_inc(cent_ps_ready, 1)
            stages(pe, stage)

        @block.scalar
        def _(act):
            def evacuate_xnT(b):
                act.wait_ge(xnT_ps, b + 1)
                need(act, v_ps, b)
                nc.scalar.activation(xnT_hi[:, :], misc[0][:, 0:L], ACT.Copy).then_inc(xnT_hi_ready, 1)

            def evacuate_qk(b, i):
                act.wait_ge(qk_ps, 4 * b + i + 1)
                if i == 0:
                    need(act, part_ready, 2 * b)
                for n in range(2):
                    g = 2 * i + n
                    nc.scalar.activation(y_qk[:, g, :], misc[(i + 1) % 2][:, n * L:(n + 1) * L], ACT.Identity,
                                         bias=bqk_sb[:, g:g + 1], scale=SCALE if g < G else 1.0).then_inc(qk_read, 1)

            def exps(s, u):
                act.wait_ge(max_ready, NU * s + u + 1)
                if u == 0:
                    need(act, att_w_done, s)
                for n in range(2):
                    tile = score_bank(u)[:, n * L:(n + 1) * L]
                    last = nc.scalar.activation(tile, tile, ACT.Exp, bias=neg_max[:, u, n:n + 1],
                                                accum_out=row_sum[:, 2 * u + n:2 * u + n + 1])
                last.then_inc(exp_done, 1)

            def gate_silu(b, e):
                act.wait_ge(gu_ps, E * b + e + 1)
                if e >= 2:
                    act.wait_ge(h_ready, E * b + e - 1)
                else:
                    need(act, h_ready, E * b + e - 1)
                for c in range(HC):
                    nc.scalar.activation(silu[:, e % 2, c, :], gu_bank(e)[0:HP, c * L:(c + 1) * L], ACT.Silu,
                                                bias=bg_sb[:, e, c:c + 1]).then_inc(silu_done, 1)

            def stage(s, par):
                has_scores, has_gu, has_y = kind(s)
                has_proj = not isinstance(s, int) or s < LAST
                if has_y:
                    act.wait_ge(delta_ready, s - 1)
                    nc.scalar.activation(e_delta[:, :], delta[:, par, :], ACT.Exp).then_inc(e_delta_ready, 1)
                for u in range(NU):
                    if has_scores:
                        exps(s, u)
                    if has_gu and u == 8:
                        act.wait_ge(x2T_ps, s)
                        need(act, gu_ps, E * (s - 1))
                        nc.scalar.activation(x2_hi[:, :], misc[0][:, 0:L], ACT.Copy).then_inc(x2_hi_ready, 1)
                    if has_proj and u == 14:
                        evacuate_xnT(s + 1)
                if isinstance(s, int) and s == 1:
                    act.wait_ge(moe_b_in, N_MOE)
                nc.scalar.preload_act_table(ACT.Silu)
                if has_proj:
                    evacuate_qk(s + 1, 0)
                    evacuate_qk(s + 1, 1)
                for e in range(E):
                    if has_gu:
                        gate_silu(s - 1, e)
                    if e == 0 and has_proj:
                        evacuate_qk(s + 1, 2)
                    if e == 1 and has_proj:
                        evacuate_qk(s + 1, 3)
                    if e == 3 and has_scores:
                        act.wait_ge(optT_ps, s + 1)
                        need(act, attn_ps, s)
                        nc.scalar.activation(optT[:, :], misc[1][:, 0:L], ACT.Copy).then_inc(optT_ready, 1)
                if not isinstance(s, int) or s <= NB:
                    nc.scalar.preload_act_table(ACT.Exp)

            evacuate_xnT(0)
            act.wait_ge(bqk_scaled, 2)
            for i in range(QK // 2):
                evacuate_qk(0, i)
            stages(act, stage)

        @block.vector
        def _(dve):
            def ln_stats(k, src, b):
                step, n = ln_step[k], 5
                for t in range(T):
                    nc.vector.bn_stats(stats[k][:, t, :], src[:, t, :]).then_inc(step, 1)
                dve.wait_ge(step, n * b + 2)
                nc.vector.memset(spare[:, :], 0.0)
                for t in range(T):
                    nc.vector.bn_aggr(mean_var[k][:, t, :], stats[k][:, t, :]).then_inc(step, 1)
                dve.wait_ge(step, n * b + 4)
                nc.vector.tensor_scalar(var_eps[k][:, :], mean_var[k][:, :, 1], EPS, None, ALU.add).then_inc(step, 1)

            def ln_scale(k, dst, src, b, done):
                dve.wait_ge(ln_rstd[k], b + 1)
                for t in range(T):
                    last = nc.vector.tensor_scalar(dst[:, t, :], src[:, t, :], mean_var[k][:, t, 0:1],
                                                   rstd[k][:, t:t + 1], ALU.subtract, ALU.mult)
                last.then_inc(done, 1)

            def norm_input_stats(b, par):
                dve.wait_ge(x_in[par], 16 * ((b - par) // 2 + 1) if isinstance(b, int) else (b - par) * 8 + 16)
                ln_stats("in", x_sb[:, par, :, :], b)

            def norm_input(b, par):
                need(dve, xnT_ps, b)
                ln_scale("in", xn, x_sb[:, par, :, :], b, xn_ready)

            def split_qk(b, side):
                grp = slice(G * side, G * side + G)
                if side:
                    need(dve, scores_ready, NU * b)
                else:
                    need(dve, q_head_ready, G * b)
                dve.wait_ge(sign_ready, 2 * b + side + 1)
                nc.vector.scalar_tensor_tensor(qk_part[:, grp, :], y_qk[:, grp, :], part_sel[:, 2 * side:2 * side + 1],
                                               y_sign[:, grp, :].bitcast(fp32), ALU.mult, ALU.add).then_inc(part_ready, 1)

            def take_v(b):
                dve.wait_ge(v_ps, b + 1)
                need(dve, opt_ready, b)
                nc.vector.tensor_tensor(v_sb[:, :, :], misc[0][:, 0:T * D].rearrange("p (t d) -> p t d", t=T),
                                        bv_sb[:, :].unsqueeze(1).to_broadcast([128, T, D]), ALU.add).then_inc(v_ready, 1)

            def row_max(s, u):
                dve.wait_ge(scores_ready, NU * s + u + 1)
                nc.vector.tensor_reduce(neg_max[:, u, :], score_bank(u).rearrange("p (n m) -> p n m", n=2),
                                        AX.X, ALU.max, negate=True).then_inc(max_ready, 1)

            def weight_values(b):
                dve.wait_ge(exp_done, NU * (b + 1))
                nc.vector.reciprocal(rec_sum[:, :], row_sum[:, :]).then_inc(rec_done, 1)
                dve.wait_ge(rec_done, b + 1)
                nc.vector.tensor_tensor(att_w[:, :], row_sum[:, :], rec_sum[:, :], ALU.mult).then_inc(att_w_done, 1)
                dve.wait_ge(att_w_done, b + 1)
                dve.wait_ge(v_ready, b + 1)
                need(dve, optT_ps, b)
                nc.vector.tensor_tensor(opt[:, :, :].rearrange("p t (h d) -> p (t h) d", d=HD),
                                        v_sb[:, :, :].rearrange("p t (h d) -> p (t h) d", d=HD),
                                        att_w[:, :].unsqueeze(2).to_broadcast([128, T * NH, HD]),
                                        ALU.mult).then_inc(opt_ready, 1)

            def take_attn(b):
                dve.wait_ge(attn_ps, b + 1)
                nc.vector.tensor_tensor(attn[:, :, :], misc[1][:, 0:T * D].rearrange("p (t d) -> p t d", t=T),
                                        bo_sb[:, :].unsqueeze(1).to_broadcast([128, T, D]), ALU.add).then_inc(attn_ready, 1)
                dve.wait_ge(attn_ready, b + 1)
                ln_stats("attn", attn, b)

            def add_attn(b, par):
                ln_scale("attn", attn_n, attn, b, attn_n_ready)
                dve.wait_ge(attn_n_ready, b + 1)
                need(dve, out_ready, b - 1)
                nc.vector.tensor_tensor(x1[:, par, :, :], x_sb[:, par, :, :], attn_n[:, :, :], ALU.add).then_inc(x1_ready, 1)
                dve.wait_ge(x1_ready, b + 1)
                ln_stats("mid", x1[:, par, :, :], b)

            def norm_mid(b, par):
                need(dve, x2T_ps, b)
                ln_scale("mid", x2, x1[:, par, :, :], b, x2_ready)
                dve.wait_ge(x2_ready, b + 1)
                need(dve, dist_step, 2 * b)
                for t in range(T):
                    last = nc.vector.scalar_tensor_tensor(x2_junk[:, t, :], x2[:, t, :], 1.0, x2[:, t, :],
                                                          ALU.mult, ALU.mult, accum_out=x2_norm[:, t:t + 1])
                last.then_inc(x2_norm_done, 1)

            def rest_of_x2(b):
                dve.wait_ge(x2_hi_ready, b + 1)
                nc.vector.tensor_tensor(x2_lo[:, :], misc[0][:, 0:L], x2_hi[:, :].bitcast(fp32), ALU.subtract)\
                    .then_inc(x2_lo_ready, 1)

            def rest_of_xnT(b):
                dve.wait_ge(xnT_hi_ready, b + 1)
                nc.vector.tensor_tensor(xnT_lo[:, :], misc[0][:, 0:L], xnT_hi[:, :].bitcast(fp32), ALU.subtract)\
                    .then_inc(xnT_lo_ready, 1)

            def square_distance(b):
                dve.wait_ge(dot_ps, b + 1)
                dve.wait_ge(x2_norm_done, b + 1)
                nc.vector.scalar_tensor_tensor(dot_d[:, :, :], misc[1][:, 0:T * E].rearrange("p (t e) -> p t e", t=T),
                                               -2.0, cent_norm[:, :, :], ALU.mult, ALU.add).then_inc(dot_read, 1)
                dve.wait_ge(dot_read, b + 1)
                nc.vector.tensor_tensor(dist_sum[:, :, :], dot_d[:, :, :],
                                        x2_norm[:, :].unsqueeze(2).to_broadcast([128, T, E]), ALU.add).then_inc(dist_step, 1)
                dve.wait_ge(dist_step, 2 * b + 1)
                nc.vector.tensor_scalar(dist_sq[:, :, :], dist_sum[:, :, :], 1e-12, None, ALU.max).then_inc(dist_step, 1)

            def route(b, par):
                dve.wait_ge(dist_ready, b + 1)
                nc.vector.memset(spare[:, :], 0.0)
                for t in range(T):
                    nc.vector.max(top[:, t, :], dist[:, t, :]).then_inc(route_step, 1)
                dve.wait_ge(route_step, 6 * b + 2)
                nc.vector.tensor_tensor(delta[:, par, :], top[:, :, 1], top[:, :, 0], ALU.subtract).then_inc(delta_ready, 1)
                for t in range(T):
                    nc.vector.max_index(top_idx[:, t, :], top[:, t, :], dist[:, t, :]).then_inc(route_step, 1)
                dve.wait_ge(route_step, 6 * b + 4)
                nc.vector.tensor_copy(top_idf[:, :, :], top_idx[:, :, 0:2]).then_inc(route_step, 1)
                dve.wait_ge(route_step, 6 * b + 5)
                for k in range(2):
                    last = nc.vector.tensor_tensor(pick[:, par, k, :, :], iota[:, :, :],
                                                   top_idf[:, :, k:k + 1].to_broadcast([128, T, E]), ALU.is_equal)
                last.then_inc(route_step, 1)

            def expert_weights(b, par):
                dve.wait_ge(e_delta_ready, b + 1)
                nc.vector.tensor_scalar(den[:, :], e_delta[:, :], 1.0, None, ALU.add).then_inc(we_step, 1)
                dve.wait_ge(we_step, 4 * b + 1)
                nc.vector.reciprocal(w_top[:, 0, :], den[:, :]).then_inc(we_step, 1)
                dve.wait_ge(we_step, 4 * b + 2)
                nc.vector.tensor_tensor(w_top[:, 1, :], e_delta[:, :], w_top[:, 0, :], ALU.mult).then_inc(we_step, 1)
                dve.wait_ge(we_step, 4 * b + 3)
                dve.wait_ge(route_step, 6 * b + 6)
                for k in range(2):
                    last = nc.vector.tensor_tensor(w_pick[:, k, :, :], pick[:, par, k, :, :],
                                                   w_top[:, k, :].unsqueeze(2).to_broadcast([128, T, E]), ALU.mult)
                last.then_inc(we_step, 1)
                dve.wait_ge(we_step, 4 * b + 4)
                nc.vector.tensor_tensor(we[:, :, :].rearrange("p e t -> p t e"), w_pick[:, 0, :, :], w_pick[:, 1, :, :], ALU.add).then_inc(we_ready, 1)

            def hidden(b, e):
                if e == 0:
                    need(dve, y_ps, (E // 2) * b)
                for c in range(HC):
                    dve.wait_ge(silu_done, (E * b + e) * HC + c + 1)
                    last = nc.vector.scalar_tensor_tensor(h_sb[0:HP, e, c, :],
                                                          gu_bank(e)[0:HP, UP_AT[c] * L:(UP_AT[c] + 1) * L],
                                                          b1_sb[:, e, c:c + 1], silu[:, e % 2, c, :], ALU.add, ALU.mult)
                last.then_inc(h_ready, 1)

            def weight_outputs(b, pair):
                dve.wait_ge(y_ps, (E // 2) * b + pair + 1)
                if pair == 0:
                    dve.wait_ge(we_ready, b + 1)
                if pair >= 2:
                    dve.wait_ge(acc_step, (E - 1) * b + 2 * pair - 3)
                nc.vector.tensor_tensor(y_w[:, pair % 2, :, :, :].rearrange("p a t d -> p (a t) d"),
                                        y_bank(pair).rearrange("p (a d) -> p a d", d=D),
                                        we[:, 2 * pair:2 * pair + 2, :].rearrange("p a t -> p (a t)").unsqueeze(2)
                                        .to_broadcast([128, 2 * T, D]),
                                        ALU.mult).then_inc(y_w_ready, 1)

            def finish_stats(b):
                dve.wait_ge(acc_step, (E - 1) * (b + 1))
                ln_stats("moe", acc[:, :].rearrange("p (t d) -> p t d", t=T), b)

            def finish_scale(b, par):
                need(dve, out_ready, b)
                ln_scale("moe", acc_n, acc[:, :].rearrange("p (t d) -> p t d", t=T), b, acc_n_ready)

            def stage(s, par):
                has_scores, has_gu, has_y = kind(s)
                has_proj = not isinstance(s, int) or s < LAST
                for u in range(NU):
                    if has_scores:
                        row_max(s, u)
                    if isinstance(s, int) and s == 0:
                        split_weights(u % 2, u // 2)
                    if has_gu and u == 3:
                        norm_mid(s - 1, 1 - par)
                    if has_y and u == 5:
                        expert_weights(s - 2, par)
                    if has_proj and u == 6:
                        norm_input_stats(s + 1, 1 - par)
                    if has_y and u in (7, 11, 14):
                        weight_outputs(s - 2, (7, 11, 14).index(u))
                    if has_proj and u == 9:
                        norm_input(s + 1, 1 - par)
                    if has_gu and u == 12:
                        rest_of_x2(s - 1)
                if has_gu:
                    square_distance(s - 1)
                if has_proj:
                    rest_of_xnT(s + 1)
                if has_y:
                    weight_outputs(s - 2, 3)
                if has_scores:
                    weight_values(s)
                if isinstance(s, int) and s == 1:
                    dve.wait_ge(moe_b_in, N_MOE)
                for e in range(E):
                    if has_gu:
                        hidden(s - 1, e)
                    if e == 0 and has_y:
                        finish_stats(s - 2)
                    if e == 1 and has_y:
                        finish_scale(s - 2, par)
                    if e == 2 and has_gu:
                        route(s - 1, 1 - par)
                    if e == 2 and has_proj:
                        split_qk(s + 1, 0)
                    if e == 3 and has_proj:
                        split_qk(s + 1, 1)
                    if e == 4 and has_proj:
                        take_v(s + 1)
                    if e == 5 and has_scores:
                        take_attn(s)
                    if e == 6 and has_scores:
                        add_attn(s, par)

            def split_weights(m, e):
                if e == 0:
                    dve.wait_ge(w_raw_in[m], 16)
                nc.vector.tensor_copy(w_hi[m][:, e, :], w_raw[m][:, e, :]).then_inc(w_hi_done, 1)
                dve.wait_ge(w_hi_done, 2 * e + m + 1)
                nc.vector.tensor_tensor(w_lo[m][:, e, :], w_raw[m][:, e, :], w_hi[m][:, e, :].bitcast(fp32),
                                        ALU.subtract).then_inc(w_lo_done, 1)

            norm_input_stats(0, 0)
            norm_input(0, 0)
            dve.wait_ge(qk_w_in, N_QK)
            half = (QK + 1) // 2
            for n, grp in enumerate((slice(0, half), slice(half, QK + 1))):
                nc.vector.tensor_copy(wqkv_hi[:, grp, :], wqkv_raw[:, grp, :]).then_inc(wqkv_hi_done, 1)
                dve.wait_ge(wqkv_hi_done, n + 1)
                nc.vector.tensor_tensor(wqkv_lo[:, grp, :], wqkv_raw[:, grp, :], wqkv_hi[:, grp, :].bitcast(fp32),
                                        ALU.subtract).then_inc(wqkv_lo_done, 1)
                if n == 0:
                    rest_of_xnT(0)
                    nc.vector.tensor_scalar(bqk_sb[:, 0:G], bqk_raw[:, 0:G], SCALE, None, ALU.mult).then_inc(bqk_scaled, 1)
                    nc.vector.tensor_copy(bqk_sb[:, G:QK], bqk_raw[:, G:QK]).then_inc(bqk_scaled, 1)
            dve.wait_ge(proj_w_in, N_PROJ)
            nc.vector.tensor_tensor(cent_sq[:, :], cent_sb[:, :], cent_sb[:, :], ALU.mult).then_inc(cent_sq_done, 1)
            nc.vector.tensor_copy(cent_hi[:, :], cent_sb[:, :]).then_inc(cent_hi_done, 1)
            dve.wait_ge(cent_hi_done, 1)
            nc.vector.tensor_tensor(cent_lo[:, :], cent_sb[:, :], cent_hi[:, :].bitcast(fp32), ALU.subtract)\
                .then_inc(cent_lo_done, 1)
            dve.wait_ge(consts_in, N_CONST)
            split_qk(0, 0)
            split_qk(0, 1)
            take_v(0)
            dve.wait_ge(cent_ps_ready, 1)
            for t in range(T):
                nc.vector.tensor_copy(cent_norm[:, t, :], misc[1][:, 0:E]).then_inc(cent_norm_done, 1)
            stages(dve, stage)

        @block.gpsimd
        def _(pool):
            def ln_root(k, b):
                pool.wait_ge(ln_step[k], 5 * b + 5)
                nc.gpsimd.tensor_tensor(rstd[k][:, :], var_eps[k][:, :], rsqrt_pow[:, :], ALU.pow).then_inc(ln_rstd[k], 1)

            def mask_heads(b, g):
                pool.wait_ge(part_ready, 2 * b + 1)
                if g == 0:
                    need(pool, scores_ready, NU * b)
                nc.gpsimd.tensor_tensor(q_head[:, g, :, :],
                                        qk_part[:, g, :].bitcast(fp32).unsqueeze(1).to_broadcast([128, 4, L]),
                                        head_sel[:, :].unsqueeze(2).to_broadcast([128, 4, L]),
                                        ALU.mult).then_inc(q_head_ready, 1)

            def sign_qk(b, side):
                pool.wait_ge(qk_read, 8 * b + 4 * (side + 1))
                need(pool, part_ready, 2 * b)
                grp = slice(G * side, G * side + G)
                nc.gpsimd.tensor_tensor(y_sign[:, grp, :], y_qk[:, grp, :],
                                        part_sel[:, 2 * side + 1:2 * side + 2].unsqueeze(2)
                                        .to_broadcast([128, G, L]), ALU.mult).then_inc(sign_ready, 1)

            def add_moe(b, par):
                pool.wait_ge(acc_n_ready, b + 1)
                if isinstance(b, int):
                    need(pool, out_sent, 16 * b)
                nc.gpsimd.tensor_tensor(out_sb[:, par, :, :], x1[:, par, :, :], acc_n[:, :, :], ALU.add)\
                    .then_inc(out_ready, 1)

            def accumulate(b, pair):
                pool.wait_ge(y_w_ready, (E // 2) * b + pair + 1)
                ya = [y_w[:, pair % 2, a, :, :].rearrange("p t d -> p (t d)") for a in range(2)]
                if pair == 0:
                    nc.gpsimd.tensor_tensor(acc[:, :], ya[0], ya[1], ALU.add).then_inc(acc_step, 1)
                else:
                    for a in range(2):
                        pool.wait_ge(acc_step, (E - 1) * b + 2 * pair - 1 + a)
                        nc.gpsimd.tensor_tensor(acc[:, :], acc[:, :], ya[a], ALU.add).then_inc(acc_step, 1)

            def stage(s, par):
                has_scores, has_gu, has_y = kind(s)
                has_proj = not isinstance(s, int) or s < LAST
                for pair in range(E // 2):
                    if has_proj and pair == 0:
                        ln_root("in", s + 1)
                    if has_y:
                        accumulate(s - 2, pair)
                if has_gu:
                    pool.wait_ge(dist_step, 2 * s)
                    nc.gpsimd.tensor_tensor(dist[:, :, :], dist_sq[:, :, :], half_pow[:, :, :], ALU.pow)\
                        .then_inc(dist_ready, 1)
                if has_y:
                    ln_root("moe", s - 2)
                if has_proj:
                    sign_qk(s + 1, 0)
                if has_y:
                    add_moe(s - 2, par)
                if has_proj:
                    sign_qk(s + 1, 1)
                    mask_heads(s + 1, 0)
                if has_scores:
                    ln_root("attn", s)
                if has_proj:
                    mask_heads(s + 1, 1)
                if has_scores:
                    ln_root("mid", s)
                if has_proj:
                    mask_heads(s + 1, 2)
                    mask_heads(s + 1, 3)

            nc.gpsimd.memset(rsqrt_pow[:, :], -0.5).then_inc(fills, 1)
            nc.gpsimd.memset(half_pow[:, :, :], 0.5).then_inc(fills, 1)
            nc.gpsimd.memset(ones[:, :], 1.0).then_inc(fills, 1)
            nc.gpsimd.memset(h_sb[:, :, 0, :], 1.0).then_inc(fills, 1)
            pool.wait_ge(fills, 2)
            ln_root("in", 0)
            pool.wait_ge(consts_in, N_CONST)
            sign_qk(0, 0)
            sign_qk(0, 1)
            for g in range(G):
                mask_heads(0, g)
            stages(pool, stage)


def kernel(L0_attn_x, L0_attn_w_in, L0_attn_b_in, L0_attn_w_out, L0_attn_b_out, L0_ffn_centroid, L0_ffn_Wg, L0_ffn_bg,
           L0_ffn_W1, L0_ffn_b1, L0_ffn_W2, L0_ffn_b2):
    import numpy as np
    import concourse.bacc as bacc
    from concourse.bass_utils import run_bass_kernel_spmd

    def arr(a):
        return np.ascontiguousarray(a)

    d, heads, experts = 128, 16, 8
    hd = d // heads
    w_in, b_in = arr(L0_attn_w_in), arr(L0_attn_b_in)
    rows = [[(4 * g + i) * 3 * hd + side * hd + k for i in range(4) for p in range(4) for k in range(hd)]
            for side in range(2) for g in range(heads // 4)]
    v_rows = [h * 3 * hd + 2 * hd + k for h in range(heads) for k in range(hd)]
    part = (np.arange(128) // hd) % 4
    lo = np.stack([part // 2, part % 2], 0)
    parts = np.stack([lo[0], 1 - 2 * lo[0], lo[1], 1 - 2 * lo[1]], 1).astype(np.float32)
    head_rows = (np.arange(128)[:, None] // 32 == np.arange(4)[None, :]).astype(np.float32)
    iota = np.tile(np.arange(experts, dtype=np.float32), (128, 2, 1))

    def chunks(bias):
        return arr(arr(bias).reshape(experts, 3, -1).transpose(2, 0, 1))

    arrays = {
        "x": arr(L0_attn_x),
        "w_qk": arr(w_in[np.array(rows)].transpose(2, 0, 1)),
        "b_qk": arr(b_in[np.array(rows)].T),
        "w_v": arr(w_in[np.array(v_rows)].T),
        "b_v": arr(np.tile(b_in[np.array(v_rows)], (128, 1))),
        "w_o": arr(arr(L0_attn_w_out).T),
        "b_o": arr(np.tile(arr(L0_attn_b_out), (128, 1))),
        "cent": arr(arr(L0_ffn_centroid).T),
        "wg": arr(L0_ffn_Wg), "bg": chunks(L0_ffn_bg), "w1": arr(L0_ffn_W1), "b1": chunks(L0_ffn_b1),
        "w2": arr(L0_ffn_W2), "b2": arr(L0_ffn_b2),
        "parts": parts, "head_rows": head_rows, "ident": np.eye(128, dtype=np.float32), "iota": iota,
    }
    nc = bacc.Bacc("TRN2", target_bir_lowering=False, num_devices=1)
    aps = [nc.dram_tensor(f"in_{n}", a.shape, mybir.dt.from_np(a.dtype), kind="ExternalInput").ap() for n, a in arrays.items()]
    out = nc.dram_tensor("out", arrays["x"].shape, mybir.dt.float32, kind="ExternalOutput").ap()
    sandwich_layer(nc, *aps, out)
    return run_bass_kernel_spmd(nc, [{f"in_{n}": a for n, a in arrays.items()}], core_ids=[0]).results[0]["out"]
```

```python
import concourse.bass as bass
from concourse import mybir
from contextlib import ExitStack


def need(eng, sem, value):
    if isinstance(value, int) and value <= 0:
        return
    eng.wait_ge(sem, value)


def sandwich_layer(nc, x, w_qk, b_qk, w_v, b_v, w_o, b_o, cent, wg, bg, w1, b1, w2, b2, parts, head_rows,
                   ident_in, iota_in, out):
    fp32, fp32r, u32 = mybir.dt.float32, mybir.dt.float32r, mybir.dt.uint32
    ALU, ACT, AX = mybir.AluOpType, mybir.ActivationFunctionType, mybir.AxisListType

    NB, L, D = x.shape
    T = L // 128
    E, _, H = wg.shape
    HC = 3
    HP = H // HC
    NH = 16
    HD = D // NH
    G = 4
    NU = NH * T // 2
    QK = 2 * G
    SCALE = float(HD) ** -0.5
    EPS = 1e-5
    LAST = NB - 1
    YW_AT = (5, 8, 12)

    ctx = ExitStack()
    with ctx:
        def sb(name, shape, dt=fp32):
            return ctx.enter_context(nc.sbuf_tensor(name, shape, dt))

        def sem(name):
            return ctx.enter_context(nc.semaphore(name))

        ident = sb("ident", [128, 128])
        iota = sb("iota", [128, T, E])
        part_sel = sb("part_sel", [128, 4])
        head_sel = sb("head_sel", [128, 4])
        wqkv_raw = sb("wqkv_raw", [128, QK + 1, 128])
        wqkv_hi = sb("wqkv_hi", [128, QK + 1, 128], fp32r)
        wqkv_lo = sb("wqkv_lo", [128, QK + 1, 128], fp32r)
        bqk_raw = sb("bqk_raw", [128, QK])
        bqk_sb = sb("bqk_sb", [128, QK])
        bv_sb = sb("bv_sb", [128, D])
        wo_sb = sb("wo_sb", [128, D])
        bo_sb = sb("bo_sb", [128, D])
        cent_sb = sb("cent_sb", [128, E])
        cent_parts = sb("cent_parts", [128, 2, E], fp32r)
        cent_sq = sb("cent_sq", [128, E])
        ones = sb("ones", [128, 128])
        cent_norm = sb("cent_norm", [128, T, E])
        w_raw = [sb(f"w_raw{i}", [128, E, H]) for i in range(2)]
        w_hi = [sb(f"w_hi{i}", [128, E, H], fp32r) for i in range(2)]
        w_lo = [sb(f"w_lo{i}", [128, E, H], fp32r) for i in range(2)]
        bg_sb = sb("bg_sb", [HP, E, HC])
        b1_sb = sb("b1_sb", [HP, E, HC])
        w2_sb = sb("w2_sb", [HP + 1, E, HC, D])
        half_pow = sb("half_pow", [128, T, E])
        minus_one = sb("minus_one", [128, T])
        rsqrt_pow = sb("rsqrt_pow", [128, T])

        x_ln = sb("x_ln", [128, 2, T, D])
        x_res = sb("x_res", [128, T, D])
        xn = sb("xn", [128, T, D])
        xnT_hi = sb("xnT_hi", [128, L], fp32r)
        xnT_lo = sb("xnT_lo", [128, L], fp32r)
        y_qk = sb("y_qk", [128, QK, L])
        y_sign = sb("y_sign", [128, QK, L], fp32r)
        qk_part = sb("qk_part", [128, QK, L], fp32r)
        q_head = sb("q_head", [128, G, 4, L], fp32r)
        v_sb = sb("v_sb", [128, T, D])
        neg_max = sb("neg_max", [128, NU, 2])
        row_sum = sb("row_sum", [128, T * NH])
        rec_sum = sb("rec_sum", [128, T * NH])
        att_w = sb("att_w", [128, T * NH])
        opt = sb("opt", [128, T, D])
        optT = sb("optT", [128, L])
        attn = sb("attn", [128, T, D])
        attn_n = sb("attn_n", [128, T, D])
        x1 = sb("x1", [128, 2, T, D])
        x2 = sb("x2", [128, T, D])
        x2_junk = sb("x2_junk", [128, T, D])
        x2_norm = sb("x2_norm", [128, T])
        x2_hi = sb("x2_hi", [128, L], fp32r)
        x2_lo = sb("x2_lo", [128, L], fp32r)
        dot_hi = sb("dot_hi", [128, T, E])
        dot_lo = sb("dot_lo", [128, T, E])
        dist_sum = sb("dist_sum", [128, T, E])
        dist_sq = sb("dist_sq", [128, T, E])
        dist = sb("dist", [128, T, E])
        top = sb("top", [128, T, 8])
        top_idx = sb("top_idx", [128, T, 8], u32)
        top_idf = sb("top_idf", [128, T, 2])
        pick = sb("pick", [128, 2, 2, T, E])
        delta = sb("delta", [128, 2, T])
        e_delta = sb("e_delta", [128, T])
        den = sb("den", [128, T])
        w_top = sb("w_top", [128, 2, T])
        w_pick = sb("w_pick", [128, 2, T, E])
        we = sb("we", [128, E, T])
        silu = sb("silu", [HP, 2, HC, L])
        h_sb = sb("h_sb", [128, E, HC, L])
        y_w = sb("y_w", [128, 2, 2, T, D])
        acc = sb("acc", [128, T * D])
        acc_n = sb("acc_n", [128, T, D])
        spare = sb("spare", [128, 1])
        pool_spare = sb("pool_spare", [128, 1])
        out_sb = sb("out_sb", [128, 2, T, D])
        stats = {k: sb(f"stats_{k}", [128, T, 6]) for k in ("in", "attn", "mid", "moe")}
        mean_var = {k: sb(f"mean_var_{k}", [128, T, 2]) for k in ("in", "attn", "mid", "moe")}
        var_eps = {k: sb(f"var_eps_{k}", [128, T]) for k in ("in", "attn", "mid", "moe")}
        rstd = {k: sb(f"rstd_{k}", [128, T]) for k in ("in", "attn", "mid", "moe")}

        psum = ctx.enter_context(nc.psum_tensor("psum", [128, 8, 512], fp32))
        misc = [psum[:, 6, :], psum[:, 7, :]]

        def gu_bank(e):
            return psum[:, 3 * (e % 2):3 * (e % 2) + 3, :].rearrange("p a b -> p (a b)")

        UP_AT = (4, 5, 3)

        def score_bank(u):
            return psum[:, (0, 1, 3, 4)[u % 4], :]

        def y_bank(pair):
            return psum[:, 2 + 3 * (pair % 2), :]

        consts_in = sem("consts_in")
        ident_in_sem = sem("ident_in_sem")
        qk_w_in = sem("qk_w_in")
        proj_w_in = sem("proj_w_in")
        w_raw_in = [sem("w_gate_in"), sem("w_up_in")]
        moe_b_in = sem("moe_b_in")
        moe_w2_in = sem("moe_w2_in")
        x_in = [sem("x_in0"), sem("x_in1")]
        res_in = sem("res_in")
        out_sent = sem("out_sent")
        fills = sem("fills")
        bqk_scaled = sem("bqk_scaled")
        cent_sq_done = sem("cent_sq_done")
        cent_ps_ready = sem("cent_ps_ready")
        cent_norm_done = sem("cent_norm_done")
        w_hi_done = sem("w_hi_done")
        w_lo_done = sem("w_lo_done")
        ln_step = {k: sem(f"ln_step_{k}") for k in ("in", "attn", "mid", "moe")}
        ln_rstd = {k: sem(f"ln_rstd_{k}") for k in ("in", "attn", "mid", "moe")}
        xn_ready = sem("xn_ready")
        xnT_ps = sem("xnT_ps")
        xnT_hi_ready = sem("xnT_hi_ready")
        xnT_lo_ready = sem("xnT_lo_ready")
        wqkv_hi_done = sem("wqkv_hi_done")
        wqkv_lo_done = sem("wqkv_lo_done")
        cent_hi_done = sem("cent_hi_done")
        cent_lo_done = sem("cent_lo_done")
        qk_ps = sem("qk_ps")
        qk_read = sem("qk_read")
        sign_ready = sem("sign_ready")
        part_ready = sem("part_ready")
        q_head_ready = sem("q_head_ready")
        first_masks_ready = sem("first_masks_ready")
        first_sign_ready = sem("first_sign_ready")
        v_ps = sem("v_ps")
        v_ready = sem("v_ready")
        scores_ready = sem("scores_ready")
        max_ready = sem("max_ready")
        exp_done = sem("exp_done")
        rec_done = sem("rec_done")
        att_w_done = sem("att_w_done")
        opt_ready = sem("opt_ready")
        optT_ps = sem("optT_ps")
        optT_ready = sem("optT_ready")
        attn_ps = sem("attn_ps")
        attn_ready = sem("attn_ready")
        attn_n_ready = sem("attn_n_ready")
        x1_ready = sem("x1_ready")
        x2_ready = sem("x2_ready")
        x2_norm_done = sem("x2_norm_done")
        x2T_ps = sem("x2T_ps")
        x2_hi_ready = sem("x2_hi_ready")
        x2_lo_ready = sem("x2_lo_ready")
        dot_ps = sem("dot_ps")
        dot_read = sem("dot_read")
        dist_step = sem("dist_step")
        dist_ready = sem("dist_ready")
        route_step = sem("route_step")
        delta_ready = sem("delta_ready")
        e_delta_ready = sem("e_delta_ready")
        we_step = sem("we_step")
        we_ready = sem("we_ready")
        gu_ps = sem("gu_ps")
        silu_done = sem("silu_done")
        h_ready = sem("h_ready")
        y_ps = sem("y_ps")
        y_w_ready = sem("y_w_ready")
        acc_step = sem("acc_step")
        acc_n_ready = sem("acc_n_ready")
        out_ready = sem("out_ready")

        N_CONST, N_QK, N_PROJ, N_MOE, N_W2 = 3 * 16, 3 * 16, 4 * 16, 2 * 16, 2 * 16

        block = ctx.enter_context(nc.Block())

        def stages(eng, first_stage, stage):
            first_stage()
            stage(1, 1)
            with eng.Fori(1, NB // 2 - 1) as r:
                stage(2 * r, 0)
                stage(2 * r + 1, 1)
            for s in range(NB - 2, NB + 2):
                stage(s, s % 2)

        def kind(s):
            if not isinstance(s, int):
                return True, True, True, True, True
            return s < NB, s <= NB, s >= 2, s < LAST, s < LAST - 1

        @block.sync
        def _(sp):
            sp.dma_start(x_ln[:, 0, :, :], x[0].rearrange("(p t) d -> p t d", p=128)).then_inc(x_in[0], 16)
            sp.dma_start(ident[:, :], ident_in).then_inc(ident_in_sem, 16)
            sp.dma_start(wqkv_raw[:, 0:QK, :], w_qk).then_inc(qk_w_in, 16)
            sp.dma_start(wqkv_raw[:, QK, :], w_v).then_inc(qk_w_in, 16)
            sp.dma_start(bqk_raw[:, :], b_qk).then_inc(qk_w_in, 16)
            sp.dma_start(part_sel[:, :], parts).then_inc(consts_in, 16)
            sp.dma_start(head_sel[:, :], head_rows).then_inc(consts_in, 16)
            sp.dma_start(iota[:, :, :], iota_in).then_inc(consts_in, 16)
            sp.dma_start(bv_sb[:, :], b_v).then_inc(proj_w_in, 16)
            sp.dma_start(x_ln[:, 1, :, :], x[1].rearrange("(p t) d -> p t d", p=128)).then_inc(x_in[1], 16)
            sp.dma_start(x_res[:, :, :], x[0].rearrange("(p t) d -> p t d", p=128)).then_inc(res_in, 16)
            sp.dma_start(wo_sb[:, :], w_o).then_inc(proj_w_in, 16)
            sp.dma_start(bo_sb[:, :], b_o).then_inc(proj_w_in, 16)
            sp.dma_start(cent_sb[:, :], cent).then_inc(proj_w_in, 16)
            sp.dma_start(w_raw[0][:, :, :], wg.rearrange("e d h -> d e h")).then_inc(w_raw_in[0], 16)
            sp.dma_start(w_raw[1][:, :, :], w1.rearrange("e d h -> d e h")).then_inc(w_raw_in[1], 16)
            sp.dma_start(bg_sb[:, :, :], bg).then_inc(moe_b_in, 16)
            sp.dma_start(b1_sb[:, :, :], b1).then_inc(moe_b_in, 16)
            sp.dma_start(w2_sb[0:HP, :, :, :], w2.rearrange("e (c p) d -> p e c d", p=HP)).then_inc(moe_w2_in, 16)
            sp.dma_start(w2_sb[HP:HP + 1, :, 0, :], b2.rearrange("(a e) d -> a e d", a=1)).then_inc(moe_w2_in, 16)

            def load(b, par):
                need(sp, xn_ready, b - 1)
                sp.dma_start(x_ln[:, par, :, :],
                             x[bass.ds(b, 1), :, :].rearrange("b (p t) d -> p (b t) d", p=128)).then_inc(x_in[par], 16)

            def load_residual(b):
                need(sp, x1_ready, b)
                sp.dma_start(x_res[:, :, :],
                             x[bass.ds(b, 1), :, :].rearrange("b (p t) d -> p (b t) d", p=128)).then_inc(res_in, 16)

            def store(b, par):
                need(sp, out_ready, b + 1)
                sp.dma_start(out[bass.ds(b, 1), :, :].rearrange("b (p t) d -> p (b t) d", p=128),
                             out_sb[:, par, :, :]).then_inc(out_sent, 16)

            def turn(st, par):
                if not isinstance(st, int) or st <= LAST - 2:
                    load(st + 2, par)
                if not isinstance(st, int) or st >= 2:
                    store(st - 2, par)
                if not isinstance(st, int) or st < LAST:
                    if not isinstance(st, int):
                        sp.wait_ge(out_sent, 16 * (st - 1))
                    load_residual(st + 1)

            stages(sp, lambda: turn(0, 0), turn)
            sp.wait_ge(out_sent, 16 * NB)

        @block.tensor
        def _(pe):
            def transpose_rows(bank, rows, done):
                for t in range(T):
                    last = nc.tensor.transpose(bank[:, t * 128:(t + 1) * 128], rows[:, t, :], ident[:, :])
                last.then_inc(done, 1)

            def product(dst, sta_hi, sta_lo, mov_hi, mov_lo):
                nc.tensor.matmul(dst, sta_hi, mov_hi, start=True, stop=False)
                nc.tensor.matmul(dst, sta_hi, mov_lo, start=False, stop=False)
                return nc.tensor.matmul(dst, sta_lo, mov_hi, start=False, stop=True)

            def project_transpose(b):
                need(pe, xn_ready, b + 1)
                transpose_rows(misc[0], xn, xnT_ps)

            def project_qk(b, i):
                if i >= 2:
                    pe.wait_ge(qk_read, 8 * b + 2 * (i - 1))
                for n in range(2):
                    last = product(misc[i % 2][:, n * L:(n + 1) * L], wqkv_hi[:, 2 * i + n, :],
                                   wqkv_lo[:, 2 * i + n, :], xnT_hi[:, :], xnT_lo[:, :])
                last.then_inc(qk_ps, 1)

            def project_v(b):
                pe.wait_ge(qk_read, 8 * b + 6)
                for t in range(T):
                    rows = slice(t * 128, (t + 1) * 128)
                    last = product(misc[0][:, t * D:(t + 1) * D], xnT_hi[:, rows], xnT_lo[:, rows],
                                   wqkv_hi[:, QK, :], wqkv_lo[:, QK, :])
                last.then_inc(v_ps, 1)

            def scores(s, u):
                t, g, half = u // (2 * G), u // 2 % G, u % 2
                if u == 0:
                    pe.wait_ge(part_ready, 4 * s + 4)
                if t == 0 and half == 0:
                    if isinstance(s, int) and s == 0 and g == 0:
                        pe.wait_ge(first_masks_ready, 1)
                    else:
                        pe.wait_ge(q_head_ready, G * s + g)
                if u < 4 and not (isinstance(s, int) and s < 2):
                    pe.wait_ge(h_ready, E * (s - 2) + E - 1 + u // 2)
                else:
                    need(pe, exp_done, NU * s + u - 3)
                for n in range(2):
                    last = nc.tensor.matmul(score_bank(u)[:, n * L:(n + 1) * L],
                                            q_head[:, g, 2 * half + n, t * 128:(t + 1) * 128], qk_part[:, G + g, :],
                                            start=True, stop=True)
                last.then_inc(scores_ready, 1)

            def second_product(b, e):
                if e == 0:
                    pe.wait_ge(h_ready, E * b + E - 1)
                elif e == 2:
                    pe.wait_ge(h_ready, E * b + E)
                if e % 2 == 0 and e >= 4:
                    pe.wait_ge(y_w_ready, (E // 2) * b + e // 2 - 1)
                for t in range(T):
                    for c in range(HC):
                        k = HP + (c == 0)
                        last = nc.tensor.matmul(y_bank(e // 2)[:, ((e % 2) * T + t) * D:((e % 2) * T + t + 1) * D],
                                                h_sb[0:k, e, c, t * 128:(t + 1) * 128], w2_sb[0:k, e, c, :],
                                                start=(c == 0), stop=(c == HC - 1))
                if e % 2:
                    last.then_inc(y_ps, 1)

            def gate_up(b, e):
                if e < 2:
                    pe.wait_ge(exp_done, NU * (LAST + 1) if isinstance(b, int) and b == LAST
                               else NU * (b + 2) - 2 + 2 * e)
                    need(pe, y_w_ready, (E // 2) * b - 1 + e)
                if e == 0:
                    pe.wait_ge(x2_lo_ready, b + 1)
                if e >= 2:
                    pe.wait_ge(h_ready, E * b + e - 1)
                bank = gu_bank(e)
                for c in range(HC):
                    for m in range(2):
                        hi = w_hi[m][:, e, c * HP:(c + 1) * HP]
                        lo = w_lo[m][:, e, c * HP:(c + 1) * HP]
                        at = UP_AT[c] if m else c
                        dst = bank[0:HP, at * L:(at + 1) * L]
                        last = product(dst, hi, lo, x2_hi[:, :], x2_lo[:, :])
                last.then_inc(gu_ps, 1)

            def attention_transpose(s):
                pe.wait_ge(opt_ready, s + 1)
                transpose_rows(misc[1], opt, optT_ps)

            def out_projection(s):
                pe.wait_ge(optT_ready, s + 1)
                for t in range(T):
                    last = nc.tensor.matmul(misc[1][:, t * D:(t + 1) * D], optT[:, t * 128:(t + 1) * 128],
                                            wo_sb[:, :], start=True, stop=True)
                last.then_inc(attn_ps, 1)

            def units_of(e):
                return {0: (), 1: (2, 3, 4), E - 1: (NU - 1,)}.get(e, (2 * e + 1, 2 * e + 2))

            def first_stage():
                scores(0, 0)
                scores(0, 1)
                pe.wait_ge(v_ready, 1)
                project_transpose(1)
                for e in range(E):
                    for u in units_of(e):
                        scores(0, u)
                    if e == 1:
                        pe.wait_ge(xnT_lo_ready, 2)
                        pe.wait_ge(cent_norm_done, T)
                    if 1 <= e <= 4:
                        project_qk(1, e - 1)
                    if e == 5:
                        project_v(1)

            def stage(s, par):
                has_scores, has_gu, has_y, has_proj, has_ln = kind(s)
                second = isinstance(s, int) and s == 1
                very_last = isinstance(s, int) and s == NB + 1
                if has_scores:
                    scores(s, 0)
                    scores(s, 1)
                if second:
                    pe.wait_ge(qk_read, 16)
                    attention_transpose(0)
                for e in range(E):
                    if has_y:
                        second_product(s - 2, e)
                    if has_proj and e == 0:
                        pe.wait_ge(v_ready, s + 1)
                        project_transpose(s + 1)
                    if has_scores:
                        for u in units_of(e):
                            scores(s, u)
                    if second and e == 1:
                        out_projection(0)
                    if has_gu and e == (4 if second else 3):
                        pe.wait_ge(x2_ready, s)
                        if has_proj:
                            pe.wait_ge(xnT_lo_ready, s + 2)
                        elif has_scores:
                            pe.wait_ge(v_ready, s + 1)
                        transpose_rows(misc[0], x2, x2T_ps)
                    if has_gu and e == 6:
                        pe.wait_ge(x2_lo_ready, s)
                        for t in range(T):
                            rows, at = slice(t * 128, (t + 1) * 128), t * 2 * E
                            nc.tensor.matmul(misc[1][:, at:at + 2 * E], x2_hi[:, rows],
                                             cent_parts[:, :, :].rearrange("p a e -> p (a e)"), start=True, stop=False)
                            last = nc.tensor.matmul(misc[1][:, at:at + E], x2_lo[:, rows], cent_parts[:, 0, :],
                                                    start=False, stop=True)
                        last.then_inc(dot_ps, 1)
                if has_proj:
                    pe.wait_ge(xnT_lo_ready, s + 2)
                    project_qk(s + 1, 0)
                if second:
                    pe.wait_ge(moe_w2_in, N_W2)
                for e in range(E):
                    if second:
                        pe.wait_ge(w_lo_done, 2 * e + 2)
                    if has_gu:
                        gate_up(s - 1, e)
                    if e == 0 and has_proj:
                        need(pe, dot_read, s)
                        project_qk(s + 1, 1)
                    if e == 1 and has_proj:
                        project_qk(s + 1, 2)
                        project_qk(s + 1, 3)
                    if e == 2 and has_scores:
                        if has_proj:
                            pe.wait_ge(qk_read, 8 * (s + 1) + 8)
                        else:
                            pe.wait_ge(dot_read, s)
                        attention_transpose(s)
                    if e == 3 and has_proj:
                        project_v(s + 1)
                    if e == 4 and has_scores:
                        out_projection(s)

            pe.wait_ge(ident_in_sem, 16)
            project_transpose(0)
            pe.wait_ge(xnT_lo_ready, 1)
            for i in range(QK // 2):
                pe.wait_ge(wqkv_lo_done, 1 + i // 2)
                project_qk(0, i)
            project_v(0)
            pe.wait_ge(proj_w_in, N_PROJ)
            pe.wait_ge(cent_lo_done, 1)
            pe.wait_ge(cent_sq_done, 1)
            pe.wait_ge(fills, 5)
            pe.wait_ge(qk_read, 8)
            nc.tensor.matmul(misc[1][:, 0:E], ones[:, :], cent_sq[:, :], start=True, stop=True).then_inc(cent_ps_ready, 1)
            stages(pe, first_stage, stage)

        @block.scalar
        def _(act):
            def evacuate_xnT(b):
                act.wait_ge(xnT_ps, b + 1)
                need(act, v_ps, b)
                nc.scalar.activation(xnT_hi[:, :], misc[0][:, 0:L], ACT.Copy).then_inc(xnT_hi_ready, 1)

            def evacuate_qk(b, i):
                act.wait_ge(qk_ps, 4 * b + i + 1)
                if i == 0:
                    need(act, part_ready, 4 * b)
                for n in range(2):
                    g = 2 * i + n
                    nc.scalar.activation(y_qk[:, g, :], misc[i % 2][:, n * L:(n + 1) * L], ACT.Identity,
                                         bias=bqk_sb[:, g:g + 1], scale=SCALE if g < G else 1.0).then_inc(qk_read, 1)

            def exps(s, u):
                act.wait_ge(max_ready, NU * s + u + 1)
                if u == 0:
                    need(act, att_w_done, s)
                for n in range(2):
                    tile = score_bank(u)[:, n * L:(n + 1) * L]
                    last = nc.scalar.activation(tile, tile, ACT.Exp, bias=neg_max[:, u, n:n + 1],
                                                accum_out=row_sum[:, 2 * u + n:2 * u + n + 1])
                last.then_inc(exp_done, 1)

            def gate_silu(b, e):
                act.wait_ge(gu_ps, E * b + e + 1)
                if e >= 2:
                    act.wait_ge(h_ready, E * b + e - 1)
                else:
                    need(act, h_ready, E * b + e - 1)
                for c in range(HC):
                    nc.scalar.activation(silu[:, e % 2, c, :], gu_bank(e)[0:HP, c * L:(c + 1) * L], ACT.Silu,
                                                bias=bg_sb[:, e, c:c + 1]).then_inc(silu_done, 1)

            def evacuate_optT(s):
                act.wait_ge(optT_ps, s + 1)
                need(act, attn_ps, s)
                nc.scalar.activation(optT[:, :], misc[1][:, 0:L], ACT.Copy).then_inc(optT_ready, 1)

            def first_stage():
                for u in range(NU):
                    exps(0, u)
                    if u == 1:
                        evacuate_xnT(1)
                    if u in (5, 7, 9, 11):
                        evacuate_qk(1, (u - 5) // 2)

            def stage(s, par):
                has_scores, has_gu, has_y, has_proj, has_ln = kind(s)
                second = isinstance(s, int) and s == 1
                very_last = isinstance(s, int) and s == NB + 1
                if has_y:
                    act.wait_ge(delta_ready, s - 1)
                    nc.scalar.activation(e_delta[:, :], delta[:, par, :], ACT.Exp).then_inc(e_delta_ready, 1)
                for u in range(NU):
                    if has_scores:
                        exps(s, u)
                    if second and u == 1:
                        evacuate_optT(0)
                    if has_gu and u == (10 if second else 8):
                        act.wait_ge(x2T_ps, s)
                        need(act, gu_ps, E * (s - 1))
                        nc.scalar.activation(x2_hi[:, :], misc[0][:, 0:L], ACT.Copy).then_inc(x2_hi_ready, 1)
                    if has_proj and u == 3:
                        evacuate_xnT(s + 1)
                if second:
                    act.wait_ge(moe_b_in, N_MOE)
                if has_gu:
                    nc.scalar.preload_act_table(ACT.Silu)
                if has_proj:
                    evacuate_qk(s + 1, 0)
                for e in range(E):
                    if has_gu:
                        gate_silu(s - 1, e)
                    if e == 0 and has_proj:
                        evacuate_qk(s + 1, 1)
                    if e == 1 and has_proj:
                        evacuate_qk(s + 1, 2)
                        evacuate_qk(s + 1, 3)
                    if e == 3 and has_scores:
                        evacuate_optT(s)
                if has_gu:
                    nc.scalar.preload_act_table(ACT.Exp)

            evacuate_xnT(0)
            act.wait_ge(bqk_scaled, 2)
            for i in range(QK // 2):
                evacuate_qk(0, i)
            act.wait_ge(part_ready, 1)
            for j in range(4):
                last = nc.scalar.activation(q_head[:, 0, j, :], qk_part[:, 0, :].bitcast(fp32), ACT.Copy,
                                            scale=head_sel[:, j:j + 1])
            last.then_inc(first_masks_ready, 1)
            stages(act, first_stage, stage)

        @block.vector
        def _(dve):
            def ln_stats(k, src, b):
                step, n = ln_step[k], 5
                for t in range(T):
                    nc.vector.bn_stats(stats[k][:, t, :], src[:, t, :]).then_inc(step, 1)
                dve.wait_ge(step, n * b + 2)
                nc.vector.memset(spare[:, :], 0.0)
                for t in range(T):
                    nc.vector.bn_aggr(mean_var[k][:, t, :], stats[k][:, t, :]).then_inc(step, 1)
                dve.wait_ge(step, n * b + 4)
                nc.vector.tensor_scalar(var_eps[k][:, :], mean_var[k][:, :, 1], EPS, None, ALU.add).then_inc(step, 1)

            def ln_scale(k, dst, src, b, done):
                dve.wait_ge(ln_rstd[k], b + 1)
                for t in range(T):
                    last = nc.vector.tensor_scalar(dst[:, t, :], src[:, t, :], mean_var[k][:, t, 0:1],
                                                   rstd[k][:, t:t + 1], ALU.subtract, ALU.mult)
                last.then_inc(done, 1)

            def norm_input_stats(b, par):
                dve.wait_ge(x_in[par], 16 * ((b - par) // 2 + 1) if isinstance(b, int) else (b - par) * 8 + 16)
                ln_stats("in", x_ln[:, par, :, :], b)

            def norm_input(b, par):
                need(dve, xnT_ps, b)
                ln_scale("in", xn, x_ln[:, par, :, :], b, xn_ready)

            def split(groups, side, done):
                nc.vector.scalar_tensor_tensor(qk_part[:, groups, :], y_qk[:, groups, :],
                                               part_sel[:, 2 * side:2 * side + 1],
                                               y_sign[:, groups, :].bitcast(fp32), ALU.mult, ALU.add)\
                    .then_inc(part_ready, done)

            def split_qk(b, side):
                if side:
                    dve.wait_ge(scores_ready, NU * b)
                else:
                    dve.wait_ge(q_head_ready, G * b - 1)
                    if isinstance(b, int) and b == 1:
                        dve.wait_ge(first_masks_ready, 1)
                if isinstance(b, int) and b == 1 and side:
                    dve.wait_ge(first_sign_ready, 6)
                else:
                    dve.wait_ge(sign_ready, 2 * b + side - (1 if isinstance(b, int) and b == 1 else 2))
                split(slice(G * side, G * side + G), side, 2)

            def sign_pair(b, i):
                dve.wait_ge(qk_read, 8 * b + 2 * i + 2)
                groups, side = slice(2 * i, 2 * i + 2), i // 2
                nc.vector.tensor_scalar(y_sign[:, groups, :], y_qk[:, groups, :],
                                        part_sel[:, 2 * side + 1:2 * side + 2], None, ALU.mult)\
                    .then_inc(first_sign_ready, 1)

            def split_first(i):
                sign_pair(0, i)
                dve.wait_ge(first_sign_ready, i + 1)
                split(slice(2 * i, 2 * i + 2), i // 2, 1)

            def take_v(b):
                dve.wait_ge(v_ps, b + 1)
                need(dve, opt_ready, b)
                nc.vector.tensor_tensor(v_sb[:, :, :], misc[0][:, 0:T * D].rearrange("p (t d) -> p t d", t=T),
                                        bv_sb[:, :].unsqueeze(1).to_broadcast([128, T, D]), ALU.add).then_inc(v_ready, 1)

            def row_max(s, u):
                dve.wait_ge(scores_ready, NU * s + u + 1)
                nc.vector.tensor_reduce(neg_max[:, u, :], score_bank(u).rearrange("p (n m) -> p n m", n=2),
                                        AX.X, ALU.max, negate=True).then_inc(max_ready, 1)

            def weight_values(b):
                dve.wait_ge(exp_done, NU * (b + 1))
                nc.vector.reciprocal(rec_sum[:, :], row_sum[:, :]).then_inc(rec_done, 1)
                dve.wait_ge(rec_done, b + 1)
                nc.vector.tensor_tensor(att_w[:, :], row_sum[:, :], rec_sum[:, :], ALU.mult).then_inc(att_w_done, 1)
                dve.wait_ge(att_w_done, b + 1)
                dve.wait_ge(v_ready, b + 1)
                need(dve, optT_ps, b)
                nc.vector.tensor_tensor(opt[:, :, :].rearrange("p t (h d) -> p (t h) d", d=HD),
                                        v_sb[:, :, :].rearrange("p t (h d) -> p (t h) d", d=HD),
                                        att_w[:, :].unsqueeze(2).to_broadcast([128, T * NH, HD]),
                                        ALU.mult).then_inc(opt_ready, 1)

            def take_attn(b):
                dve.wait_ge(attn_ps, b + 1)
                nc.vector.tensor_tensor(attn[:, :, :], misc[1][:, 0:T * D].rearrange("p (t d) -> p t d", t=T),
                                        bo_sb[:, :].unsqueeze(1).to_broadcast([128, T, D]), ALU.add).then_inc(attn_ready, 1)
                dve.wait_ge(attn_ready, b + 1)
                ln_stats("attn", attn, b)

            def norm_attn(b):
                need(dve, x1_ready, b)
                ln_scale("attn", attn_n, attn, b, attn_n_ready)

            def mid_stats(b, par):
                dve.wait_ge(x1_ready, b + 1)
                ln_stats("mid", x1[:, par, :, :], b)

            def norm_mid(b, par):
                need(dve, x2T_ps, b)
                ln_scale("mid", x2, x1[:, par, :, :], b, x2_ready)
                dve.wait_ge(x2_ready, b + 1)
                need(dve, dist_step, 2 * b)
                for t in range(T):
                    last = nc.vector.scalar_tensor_tensor(x2_junk[:, t, :], x2[:, t, :], 1.0, x2[:, t, :],
                                                          ALU.mult, ALU.mult, accum_out=x2_norm[:, t:t + 1])
                last.then_inc(x2_norm_done, 1)

            def rest_of_x2(b):
                dve.wait_ge(x2_hi_ready, b + 1)
                nc.vector.tensor_tensor(x2_lo[:, :], misc[0][:, 0:L], x2_hi[:, :].bitcast(fp32), ALU.subtract)\
                    .then_inc(x2_lo_ready, 1)

            def rest_of_xnT(b):
                dve.wait_ge(xnT_hi_ready, b + 1)
                nc.vector.tensor_tensor(xnT_lo[:, :], misc[0][:, 0:L], xnT_hi[:, :].bitcast(fp32), ALU.subtract)\
                    .then_inc(xnT_lo_ready, 1)

            def square_distance(b):
                dve.wait_ge(dot_ps, b + 1)
                dve.wait_ge(x2_norm_done, b + 1)
                dots = misc[1][:, 0:T * 2 * E].rearrange("p (t a e) -> p t a e", t=T, a=2)
                nc.vector.scalar_tensor_tensor(dot_hi[:, :, :], dots[:, :, 0, :], -2.0, cent_norm[:, :, :],
                                               ALU.mult, ALU.add)
                nc.vector.scalar_tensor_tensor(dot_lo[:, :, :], dots[:, :, 1, :], -2.0,
                                               x2_norm[:, :].unsqueeze(2).to_broadcast([128, T, E]),
                                               ALU.mult, ALU.add).then_inc(dot_read, 1)
                dve.wait_ge(dot_read, b + 1)
                nc.vector.tensor_tensor(dist_sum[:, :, :], dot_hi[:, :, :], dot_lo[:, :, :], ALU.add)\
                    .then_inc(dist_step, 1)
                dve.wait_ge(dist_step, 2 * b + 1)
                nc.vector.tensor_scalar(dist_sq[:, :, :], dist_sum[:, :, :], 1e-12, None, ALU.max).then_inc(dist_step, 1)

            def route(b, par):
                dve.wait_ge(dist_ready, b + 1)
                nc.vector.memset(spare[:, :], 0.0)
                for t in range(T):
                    nc.vector.max(top[:, t, :], dist[:, t, :]).then_inc(route_step, 1)
                dve.wait_ge(route_step, 6 * b + 2)
                nc.vector.tensor_tensor(delta[:, par, :], top[:, :, 1], top[:, :, 0], ALU.subtract).then_inc(delta_ready, 1)
                for t in range(T):
                    nc.vector.max_index(top_idx[:, t, :], top[:, t, :], dist[:, t, :]).then_inc(route_step, 1)
                dve.wait_ge(route_step, 6 * b + 4)
                nc.vector.tensor_copy(top_idf[:, :, :], top_idx[:, :, 0:2]).then_inc(route_step, 1)
                dve.wait_ge(route_step, 6 * b + 5)
                for k in range(2):
                    last = nc.vector.tensor_tensor(pick[:, par, k, :, :], iota[:, :, :],
                                                   top_idf[:, :, k:k + 1].to_broadcast([128, T, E]), ALU.is_equal)
                last.then_inc(route_step, 1)

            def hidden(b, e):
                if e == 0:
                    need(dve, y_ps, (E // 2) * b)
                for c in range(HC):
                    dve.wait_ge(silu_done, (E * b + e) * HC + c + 1)
                    last = nc.vector.scalar_tensor_tensor(h_sb[0:HP, e, c, :],
                                                          gu_bank(e)[0:HP, UP_AT[c] * L:(UP_AT[c] + 1) * L],
                                                          b1_sb[:, e, c:c + 1], silu[:, e % 2, c, :], ALU.add, ALU.mult)
                last.then_inc(h_ready, 1)

            def weight_outputs(b, pair):
                dve.wait_ge(y_ps, (E // 2) * b + pair + 1)
                if pair == 0:
                    dve.wait_ge(we_ready, b + 1)
                if pair >= 2:
                    dve.wait_ge(acc_step, (E - 1) * b + 2 * pair - 3)
                nc.vector.tensor_tensor(y_w[:, pair % 2, :, :, :].rearrange("p a t d -> p (a t) d"),
                                        y_bank(pair).rearrange("p (a d) -> p a d", d=D),
                                        we[:, 2 * pair:2 * pair + 2, :].rearrange("p a t -> p (a t)").unsqueeze(2)
                                        .to_broadcast([128, 2 * T, D]),
                                        ALU.mult).then_inc(y_w_ready, 1)

            def add_outputs(pair):
                b = LAST
                dve.wait_ge(y_w_ready, (E // 2) * b + pair + 1)
                ya = [y_w[:, pair % 2, a, :, :].rearrange("p t d -> p (t d)") for a in range(2)]
                if pair == 0:
                    nc.vector.tensor_tensor(acc[:, :], ya[0], ya[1], ALU.add).then_inc(acc_step, 1)
                else:
                    for a in range(2):
                        dve.wait_ge(acc_step, (E - 1) * b + 2 * pair - 1 + a)
                        nc.vector.tensor_tensor(acc[:, :], acc[:, :], ya[a], ALU.add).then_inc(acc_step, 1)

            def finish_stats(b):
                dve.wait_ge(acc_step, (E - 1) * (b + 1))
                ln_stats("moe", acc[:, :].rearrange("p (t d) -> p t d", t=T), b)

            def finish_scale(b):
                need(dve, out_ready, b)
                ln_scale("moe", acc_n, acc[:, :].rearrange("p (t d) -> p t d", t=T), b, acc_n_ready)

            def round_weights(n):
                m, e = n % 2, n // 2
                if e == 0:
                    dve.wait_ge(w_raw_in[m], 16)
                nc.vector.tensor_copy(w_hi[m][:, e, :], w_raw[m][:, e, :]).then_inc(w_hi_done, 1)

            def first_stage():
                for u in range(NU):
                    row_max(0, u)
                    if 4 <= u < 14:
                        round_weights(u - 4)
                    if u == 3:
                        rest_of_xnT(1)
                    if u == 6:
                        norm_input_stats(2, 0)
                    if u == 9:
                        norm_input(2, 0)
                    if u == 11:
                        split_qk(1, 0)
                    if u == 12:
                        dve.wait_ge(part_ready, 4)
                        sign_pair(1, 2)
                    if u == 14:
                        sign_pair(1, 3)
                split_qk(1, 1)
                row_max(1, 0)
                row_max(1, 1)
                weight_values(0)
                take_v(1)

            def stage(s, par):
                has_scores, has_gu, has_y, has_proj, has_ln = kind(s)
                second = isinstance(s, int) and s == 1
                very_last = isinstance(s, int) and s == NB + 1
                for u in range(2, NU):
                    if has_scores:
                        row_max(s, u)
                    if second and u == 4:
                        take_attn(0)
                    if second and u == 6:
                        norm_attn(0)
                    if second and u == 7:
                        mid_stats(0, 0)
                    if second and 11 <= u < 15:
                        round_weights(u - 1)
                    if has_gu and u == (9 if second else 4):
                        norm_mid(s - 1, 1 - par)
                    if has_proj and u == 5:
                        rest_of_xnT(s + 1)
                    if has_y and u in YW_AT:
                        weight_outputs(s - 2, YW_AT.index(u))
                        if very_last:
                            add_outputs(YW_AT.index(u))
                    if has_gu and u == (12 if second else 10):
                        rest_of_x2(s - 1)
                if has_gu:
                    square_distance(s - 1)
                if has_y:
                    weight_outputs(s - 2, 3)
                    if very_last:
                        add_outputs(3)
                if has_scores:
                    weight_values(s)
                if has_ln:
                    norm_input_stats(s + 2, par)
                if second:
                    dve.wait_ge(moe_b_in, N_MOE)
                for e in range(E):
                    if second and e == 0:
                        round_weights(14)
                        round_weights(15)
                    if has_gu:
                        hidden(s - 1, e)
                    if e == E - 1 and has_proj:
                        row_max(s + 1, 0)
                        row_max(s + 1, 1)
                    if e == 0 and has_y:
                        finish_stats(s - 2)
                    if e == 1 and has_ln:
                        norm_input(s + 2, par)
                    if e == 1 and very_last:
                        finish_scale(s - 2)
                        dve.wait_ge(acc_n_ready, NB)
                        nc.vector.tensor_tensor(out_sb[:, par, :, :], x1[:, par, :, :], acc_n[:, :, :], ALU.add)\
                            .then_inc(out_ready, 1)
                    if e == 2 and has_gu:
                        route(s - 1, 1 - par)
                    if e in (3, 4) and has_proj:
                        split_qk(s + 1, e - 3)
                    if e == 4 and has_proj:
                        take_v(s + 1)
                    if e == 5 and has_scores:
                        take_attn(s)
                    if e == 6 and has_scores:
                        norm_attn(s)
                    if e == 7 and has_scores:
                        mid_stats(s, par)

            norm_input_stats(0, 0)
            dve.wait_ge(qk_w_in, N_QK)
            half = (QK + 1) // 2
            first_half, second_half = slice(0, half), slice(half, QK + 1)
            nc.vector.tensor_copy(wqkv_hi[:, first_half, :], wqkv_raw[:, first_half, :]).then_inc(wqkv_hi_done, 1)
            norm_input(0, 0)
            nc.vector.tensor_copy(wqkv_hi[:, second_half, :], wqkv_raw[:, second_half, :]).then_inc(wqkv_hi_done, 1)
            dve.wait_ge(wqkv_hi_done, 1)
            nc.vector.tensor_tensor(wqkv_lo[:, first_half, :], wqkv_raw[:, first_half, :],
                                    wqkv_hi[:, first_half, :].bitcast(fp32), ALU.subtract).then_inc(wqkv_lo_done, 1)
            rest_of_xnT(0)
            nc.vector.tensor_scalar(bqk_sb[:, 0:G], bqk_raw[:, 0:G], SCALE, None, ALU.mult).then_inc(bqk_scaled, 1)
            nc.vector.tensor_copy(bqk_sb[:, G:QK], bqk_raw[:, G:QK]).then_inc(bqk_scaled, 1)
            dve.wait_ge(wqkv_hi_done, 2)
            nc.vector.tensor_tensor(wqkv_lo[:, second_half, :], wqkv_raw[:, second_half, :],
                                    wqkv_hi[:, second_half, :].bitcast(fp32), ALU.subtract).then_inc(wqkv_lo_done, 1)
            norm_input_stats(1, 1)
            dve.wait_ge(consts_in, N_CONST)
            split_first(0)
            norm_input(1, 1)
            split_first(1)
            split_first(2)
            split_first(3)
            dve.wait_ge(proj_w_in, N_PROJ)
            nc.vector.tensor_tensor(cent_sq[:, :], cent_sb[:, :], cent_sb[:, :], ALU.mult).then_inc(cent_sq_done, 1)
            nc.vector.tensor_copy(cent_parts[:, 0, :], cent_sb[:, :]).then_inc(cent_hi_done, 1)
            dve.wait_ge(cent_hi_done, 1)
            nc.vector.tensor_tensor(cent_parts[:, 1, :], cent_sb[:, :], cent_parts[:, 0, :].bitcast(fp32), ALU.subtract)\
                .then_inc(cent_lo_done, 1)
            take_v(0)
            dve.wait_ge(cent_ps_ready, 1)
            for t in range(T):
                nc.vector.tensor_copy(cent_norm[:, t, :], misc[1][:, 0:E]).then_inc(cent_norm_done, 1)
            stages(dve, first_stage, stage)

        @block.gpsimd
        def _(pool):
            def ln_root(k, b):
                pool.wait_ge(ln_step[k], 5 * b + 5)
                nc.gpsimd.tensor_tensor(rstd[k][:, :], var_eps[k][:, :], rsqrt_pow[:, :], ALU.pow).then_inc(ln_rstd[k], 1)

            def mask_heads(b, g):
                pool.wait_ge(part_ready, 1 + g // 2 if isinstance(b, int) and b == 0 else 4 * b + 2)
                if not isinstance(b, int) or b > 0:
                    pool.wait_ge(scores_ready, NU * b - 2 * (G - 1 - g))
                nc.gpsimd.tensor_tensor(q_head[:, g, :, :],
                                        qk_part[:, g, :].bitcast(fp32).unsqueeze(1).to_broadcast([128, 4, L]),
                                        head_sel[:, :].unsqueeze(2).to_broadcast([128, 4, L]),
                                        ALU.mult).then_inc(q_head_ready, 1)

            def sign_qk(b, side):
                pool.wait_ge(qk_read, 8 * b + 4 * (side + 1))
                need(pool, part_ready, 4 * b)
                grp = slice(G * side, G * side + G)
                nc.gpsimd.tensor_tensor(y_sign[:, grp, :], y_qk[:, grp, :],
                                        part_sel[:, 2 * side + 1:2 * side + 2].unsqueeze(2)
                                        .to_broadcast([128, G, L]), ALU.mult).then_inc(sign_ready, 1)

            def expert_weights(b, par):
                pool.wait_ge(e_delta_ready, b + 1)
                nc.gpsimd.tensor_tensor(den[:, :], e_delta[:, :], ones[:, 0:T], ALU.add).then_inc(we_step, 1)
                pool.wait_ge(we_step, 4 * b + 1)
                nc.gpsimd.tensor_tensor(w_top[:, 0, :], den[:, :], minus_one[:, :], ALU.pow).then_inc(we_step, 1)
                pool.wait_ge(we_step, 4 * b + 2)
                nc.gpsimd.tensor_tensor(w_top[:, 1, :], e_delta[:, :], w_top[:, 0, :], ALU.mult).then_inc(we_step, 1)
                pool.wait_ge(we_step, 4 * b + 3)
                pool.wait_ge(route_step, 6 * b + 6)
                for k in range(2):
                    last = nc.gpsimd.tensor_tensor(w_pick[:, k, :, :], pick[:, par, k, :, :],
                                                   w_top[:, k, :].unsqueeze(2).to_broadcast([128, T, E]), ALU.mult)
                last.then_inc(we_step, 1)
                pool.wait_ge(we_step, 4 * b + 4)
                nc.gpsimd.tensor_tensor(we[:, :, :].rearrange("p e t -> p t e"), w_pick[:, 0, :, :],
                                        w_pick[:, 1, :, :], ALU.add).then_inc(we_ready, 1)

            def add_attn(b, par):
                pool.wait_ge(attn_n_ready, b + 1)
                pool.wait_ge(res_in, 16 * (b + 1))
                nc.gpsimd.tensor_tensor(x1[:, par, :, :], x_res[:, :, :], attn_n[:, :, :], ALU.add).then_inc(x1_ready, 1)

            def add_moe(b, par):
                pool.wait_ge(ln_rstd["moe"], b + 1)
                need(pool, out_ready, b)
                nc.gpsimd.tensor_tensor(pool_spare[:, :], ones[:, 0:1], ones[:, 1:2], ALU.mult)
                for t in range(T):
                    last = nc.gpsimd.tensor_scalar(acc_n[:, t, :], acc[:, t * D:(t + 1) * D], mean_var["moe"][:, t, 0:1],
                                                   rstd["moe"][:, t:t + 1], ALU.subtract, ALU.mult)
                last.then_inc(acc_n_ready, 1)
                pool.wait_ge(acc_n_ready, b + 1)
                if isinstance(b, int):
                    need(pool, out_sent, 16 * b)
                nc.gpsimd.tensor_tensor(out_sb[:, par, :, :], x1[:, par, :, :], acc_n[:, :, :], ALU.add)\
                    .then_inc(out_ready, 1)

            def accumulate(b, pair):
                pool.wait_ge(y_w_ready, (E // 2) * b + pair + 1)
                ya = [y_w[:, pair % 2, a, :, :].rearrange("p t d -> p (t d)") for a in range(2)]
                if pair == 0:
                    nc.gpsimd.tensor_tensor(acc[:, :], ya[0], ya[1], ALU.add).then_inc(acc_step, 1)
                else:
                    for a in range(2):
                        pool.wait_ge(acc_step, (E - 1) * b + 2 * pair - 1 + a)
                        nc.gpsimd.tensor_tensor(acc[:, :], acc[:, :], ya[a], ALU.add).then_inc(acc_step, 1)

            def rest_of_weights(first, end):
                for n in range(first, end):
                    m, e = n % 2, n // 2
                    pool.wait_ge(w_hi_done, n + 1)
                    nc.gpsimd.tensor_tensor(w_lo[m][:, e, :], w_raw[m][:, e, :], w_hi[m][:, e, :].bitcast(fp32),
                                            ALU.subtract).then_inc(w_lo_done, 1)

            def first_stage():
                rest_of_weights(0, 2)
                ln_root("in", 2)
                rest_of_weights(2, 4)
                sign_qk(1, 0)
                rest_of_weights(4, 5)
                for g in range(G):
                    mask_heads(1, g)

            def stage(s, par):
                has_scores, has_gu, has_y, has_proj, has_ln = kind(s)
                second = isinstance(s, int) and s == 1
                very_last = isinstance(s, int) and s == NB + 1
                if second:
                    ln_root("attn", 0)
                    rest_of_weights(5, 6)
                    add_attn(0, 0)
                    ln_root("mid", 0)
                    rest_of_weights(6, 14)
                if has_y:
                    if not very_last:
                        for pair in range(E // 2):
                            accumulate(s - 2, pair)
                if has_ln:
                    ln_root("in", s + 2)
                if has_gu:
                    pool.wait_ge(dist_step, 2 * s)
                    nc.gpsimd.tensor_tensor(dist[:, :, :], dist_sq[:, :, :], half_pow[:, :, :], ALU.pow)\
                        .then_inc(dist_ready, 1)
                if has_y:
                    ln_root("moe", s - 2)
                if has_proj:
                    sign_qk(s + 1, 0)
                if second:
                    rest_of_weights(14, 16)
                if has_y and not very_last:
                    add_moe(s - 2, par)
                if has_proj:
                    sign_qk(s + 1, 1)
                    for g in range(G - 1):
                        mask_heads(s + 1, g)
                if has_scores:
                    ln_root("attn", s)
                if has_proj:
                    mask_heads(s + 1, G - 1)
                if has_scores:
                    add_attn(s, par)
                if has_gu:
                    expert_weights(s - 1, 1 - par)
                if has_scores:
                    ln_root("mid", s)

            nc.gpsimd.memset(rsqrt_pow[:, :], -0.5).then_inc(fills, 1)
            nc.gpsimd.memset(half_pow[:, :, :], 0.5).then_inc(fills, 1)
            nc.gpsimd.memset(ones[:, :], 1.0).then_inc(fills, 1)
            nc.gpsimd.memset(minus_one[:, :], -1.0).then_inc(fills, 1)
            nc.gpsimd.memset(h_sb[:, :, 0, :], 1.0).then_inc(fills, 1)
            pool.wait_ge(fills, 5)
            ln_root("in", 0)
            ln_root("in", 1)
            pool.wait_ge(consts_in, N_CONST)
            for g in range(1, G):
                mask_heads(0, g)
            stages(pool, first_stage, stage)


def kernel(L0_attn_x, L0_attn_w_in, L0_attn_b_in, L0_attn_w_out, L0_attn_b_out, L0_ffn_centroid, L0_ffn_Wg, L0_ffn_bg,
           L0_ffn_W1, L0_ffn_b1, L0_ffn_W2, L0_ffn_b2):
    import numpy as np
    import concourse.bacc as bacc
    from concourse.bass_utils import run_bass_kernel_spmd

    def arr(a):
        return np.ascontiguousarray(a)

    d, heads, experts = 128, 16, 8
    hd = d // heads
    w_in, b_in = arr(L0_attn_w_in), arr(L0_attn_b_in)
    rows = [[(4 * g + i) * 3 * hd + side * hd + k for i in range(4) for p in range(4) for k in range(hd)]
            for side in range(2) for g in range(heads // 4)]
    v_rows = [h * 3 * hd + 2 * hd + k for h in range(heads) for k in range(hd)]
    part = (np.arange(128) // hd) % 4
    lo = np.stack([part // 2, part % 2], 0)
    parts = np.stack([lo[0], 1 - 2 * lo[0], lo[1], 1 - 2 * lo[1]], 1).astype(np.float32)
    head_rows = (np.arange(128)[:, None] // 32 == np.arange(4)[None, :]).astype(np.float32)
    iota = np.tile(np.arange(experts, dtype=np.float32), (128, 2, 1))

    def chunks(bias):
        return arr(arr(bias).reshape(experts, 3, -1).transpose(2, 0, 1))

    arrays = {
        "x": arr(L0_attn_x),
        "w_qk": arr(w_in[np.array(rows)].transpose(2, 0, 1)),
        "b_qk": arr(b_in[np.array(rows)].T),
        "w_v": arr(w_in[np.array(v_rows)].T),
        "b_v": arr(np.tile(b_in[np.array(v_rows)], (128, 1))),
        "w_o": arr(arr(L0_attn_w_out).T),
        "b_o": arr(np.tile(arr(L0_attn_b_out), (128, 1))),
        "cent": arr(arr(L0_ffn_centroid).T),
        "wg": arr(L0_ffn_Wg), "bg": chunks(L0_ffn_bg), "w1": arr(L0_ffn_W1), "b1": chunks(L0_ffn_b1),
        "w2": arr(L0_ffn_W2), "b2": arr(L0_ffn_b2),
        "parts": parts, "head_rows": head_rows, "ident": np.eye(128, dtype=np.float32), "iota": iota,
    }
    nc = bacc.Bacc("TRN2", target_bir_lowering=False, num_devices=1)
    aps = [nc.dram_tensor(f"in_{n}", a.shape, mybir.dt.from_np(a.dtype), kind="ExternalInput").ap() for n, a in arrays.items()]
    out = nc.dram_tensor("out", arrays["x"].shape, mybir.dt.float32, kind="ExternalOutput").ap()
    sandwich_layer(nc, *aps, out)
    return run_bass_kernel_spmd(nc, [{f"in_{n}": a for n, a in arrays.items()}], core_ids=[0]).results[0]["out"]
```
